# Optimizing a Trainium2 kernel written in Bass

```python
import numpy as np
import jax
import jax.numpy as jnp

def _softmax(x, axis=-1):
    return jax.nn.softmax(x, axis=axis)

def _gelu(x):
    return jax.nn.gelu(x, approximate=True)

def _silu(x):
    return jax.nn.silu(x)

def _sigmoid(x):
    return jax.nn.sigmoid(x)

def _layernorm(x, axis=-1, eps=1e-05):
    m = jnp.mean(x, axis=axis, keepdims=True)
    v = jnp.var(x, axis=axis, keepdims=True)
    return (x - m) / jnp.sqrt(v + eps)

def _scatter_add(tgt, idx, src, axis=0):
    return tgt.at[idx].add(src)

def _segment_sum(src, seg, n):
    return jax.ops.segment_sum(src, seg, n)
kernel_name = 'mk_gnn_resnorm_d1_gnn_r32_ecaa13'

def setup_inputs(seed: int=0):
    np.random.seed(seed)
    _w = jnp.asarray

    def _rec_inputs():
        import jax
        import jax.numpy as jnp
        _gk = jax.random.key(seed)
        x = -7.329e-05 + 0.9999 * jax.random.normal(jax.random.fold_in(_gk, 1), (50000, 512), jnp.float32)
        _s = jax.random.randint(jax.random.fold_in(_gk, 2), (12500,), 0, 50000, jnp.int32)
        _d = jax.random.randint(jax.random.fold_in(_gk, 3), (12500,), 0, 50000, jnp.int32)
        _loop = jnp.arange(50000, dtype=jnp.int32)
        src = jnp.concatenate([_s, _d, _loop])
        dst = jnp.concatenate([_d, _s, _loop])
        _o = jnp.argsort(dst, stable=True)
        src = src[_o]
        dst = dst[_o]
        return (x, src, dst)
    x, src, dst = _rec_inputs()

    def _L0_gnn_setup():
        import jax, jax.numpy as jnp
        import numpy as np
        N = 3125
        E = 25000
        D_IN = 512
        D_OUT = 512
        EPS = 1e-05
        key = jax.random.key(seed)
        k = jax.random.split(key, 7)
        x = jax.random.normal(k[0], (N, D_IN), dtype=jnp.float32)
        edge_index = jax.random.randint(k[1], (2, E), 0, N, dtype=jnp.int64)
        W_l = jax.random.normal(k[2], (D_OUT, D_IN), dtype=jnp.float32) * 0.02
        b_l = jnp.zeros((D_OUT,), dtype=jnp.float32)
        W_r = jax.random.normal(k[3], (D_OUT, D_IN), dtype=jnp.float32) * 0.02
        gamma = jnp.ones((D_OUT,), dtype=jnp.float32)
        beta = jnp.zeros((D_OUT,), dtype=jnp.float32)
        return {'x': x, 'edge_index': edge_index, 'W_l': W_l, 'b_l': b_l, 'W_r': W_r, 'gamma': gamma, 'beta': beta}
    _L0_gnn_all = _L0_gnn_setup()
    _L0_gnn_in = {k: v for k, v in _L0_gnn_all.items() if k in ('W_l', 'b_l', 'W_r', 'gamma', 'beta')}
    del _L0_gnn_all
    return {'x': x, 'src': src, 'dst': dst, 'L0_gnn_W_l': _L0_gnn_in['W_l'], 'L0_gnn_b_l': _L0_gnn_in['b_l'], 'L0_gnn_W_r': _L0_gnn_in['W_r'], 'L0_gnn_gamma': _L0_gnn_in['gamma'], 'L0_gnn_beta': _L0_gnn_in['beta']}

def reference(x, src, dst, L0_gnn_W_l, L0_gnn_b_l, L0_gnn_W_r, L0_gnn_gamma, L0_gnn_beta):
    import jax
    import jax.numpy as jnp

    def _L0_gnn_ref(x, edge_index, W_l, b_l, W_r, gamma, beta):
        import jax, jax.numpy as jnp
        import numpy as np
        N = 3125
        E = 25000
        D_IN = 512
        D_OUT = 512
        EPS = 1e-05
        n = x.shape[0]
        src, dst = (edge_index[0], edge_index[1])
        summed = jax.ops.segment_sum(x[src], dst, num_segments=n)
        cnt = jax.ops.segment_sum(jnp.ones((src.shape[0],), x.dtype), dst, num_segments=n)
        aggr = summed / jnp.maximum(cnt, 1.0)[:, None]
        h = aggr @ W_l.T + b_l + x @ W_r.T
        mu = jnp.mean(h, axis=0)
        var = jnp.mean(jnp.square(h - mu), axis=0)
        h_norm = (h - mu) * jax.lax.rsqrt(var + EPS) * gamma + beta
        return jax.nn.relu(h_norm)
    edge_index = jnp.stack([src, dst])
    x = _layernorm(x + _L0_gnn_ref(x, edge_index, L0_gnn_W_l, L0_gnn_b_l, L0_gnn_W_r, L0_gnn_gamma, L0_gnn_beta), axis=-1)
    return x

_drawn_inputs = setup_inputs


def setup_inputs(seed=0):
    import zlib

    import numpy as np

    out = dict(_drawn_inputs(seed))
    spreads = {'L0_gnn_b_l': (0.0, 0.1), 'L0_gnn_gamma': (1.0, 0.2), 'L0_gnn_beta': (0.0, 0.1)}
    factors = {}
    for name, (base, spread) in spreads.items():
        noise = np.random.default_rng([zlib.crc32(name.encode()), seed]).standard_normal(out[name].shape)
        drawn = base * np.exp(spread * noise) if base else spread * noise
        out[name] = jnp.asarray(drawn.astype(out[name].dtype))
    for name, factor in factors.items():
        out[name] = (out[name] * factor).astype(out[name].dtype)
    return out
```

```python
from contextlib import ExitStack

import concourse.bass as bass
from concourse import mybir

ALU = mybir.AluOpType
ACT = mybir.ActivationFunctionType
AX = mybir.AxisListType
F32 = mybir.dt.float32
F32R = mybir.dt.float32r
BF16 = mybir.dt.bfloat16
I32 = mybir.dt.int32
U32 = mybir.dt.uint32

P = 128
GT = 4
GR = GT * P
WIN = 3
LOOP = 2 * GT
H2 = 4
EPS = 1e-5


def largest_divisor(n, most):
    return max(k for k in range(1, most + 1) if n % k == 0)


def bass_sage_batchnorm_residual_layernorm_kernel(
    nc, x, src, dst, w_l, b_l, w_r, gamma, beta, out
):
    N, D = x.shape
    E = src.shape[0]
    KC = D // P
    TILES = -(-N // P)
    GROUPS = -(-TILES // GT)
    LAST_ROWS = N - (TILES - 1) * P
    EB = largest_divisor(E, P)
    NB = E // EB
    BP = largest_divisor(NB, P)
    BC = NB // BP
    PAIRS = (GROUPS - 1) // 2
    ROUNDS2 = (GROUPS - 1) // H2
    REST = LOOP * PAIRS
    EMPTY = 1 << 16
    assert D == KC * P and KC == GT and N < EMPTY and TILES <= 512
    assert WIN * EB >= P
    assert REST + 7 >= TILES and REST + LOOP >= GROUPS * GT - GT + 1 and PAIRS >= 1

    def rows_of(i):
        return LAST_ROWS if isinstance(i, int) and i == TILES - 1 else P

    def exists(i):
        return not isinstance(i, int) or 0 <= i < TILES

    CW = D + 8
    sum_dram = nc.dram_tensor("sum_scratch", (N, CW), F32).ap()
    mean_dram = nc.dram_tensor("mean_scratch", (N, D), F32).ap()
    h_dram = nc.dram_tensor("h_scratch", (GROUPS, P, KC, GR), F32).ap()

    def x_group(g):
        return x[bass.ds(g * GR, GR), :].rearrange("(t p) f -> p t f", p=P)

    with ExitStack() as ctx:
        def sem(name):
            return ctx.enter_context(nc.semaphore(name))

        def allocator(stack):
            return lambda name, shape, dt: stack.enter_context(nc.sbuf_tensor(name, shape, dt))

        sb = allocator(ctx)

        def ps(name, shape, dt=F32):
            return ctx.enter_context(nc.psum_tensor(name, shape, dt))

        ident = sb("ident", [P, P], F32)
        iota_m = sb("iota_m", [P, P], F32)
        iota_0 = sb("iota_0", [P, P], F32)
        iota_1 = sb("iota_1", [P, P], F32)
        ones_b = sb("ones_b", [P, P], BF16)
        ones_f = sb("ones_f", [P, 1], F32)
        left_over = sb("left_over", [P, 1], I32)
        tri = sb("tri", [P, P], BF16)
        stats = sb("stats", [P, KC, GROUPS, 6], F32)
        vec = sb("vec", [P, 3, KC], F32)
        bn_mv = sb("bn_mv", [P, KC, 2], F32)
        bn_t = sb("bn_t", [P, 3, KC], F32)
        bn_scale = sb("bn_scale", [P, KC], F32)
        bn_bias = sb("bn_bias", [P, KC], F32)
        eps_c = sb("eps_c", [P, 1], F32)

        one = ExitStack()
        s1 = allocator(one)
        wT = {(m, part): s1(f"w{m}T_{part}", [P, KC, D], F32R) for m in "lr" for part in ("hi", "lo")}
        vals = s1("vals", [P, WIN, TILES + 1, 6], BF16)
        slot1 = s1("slot1", [P, WIN, TILES + 1], F32)
        dl = s1("dl", [P, WIN, TILES + 1], F32)

        zero = ExitStack()
        s0 = allocator(zero)
        w_nat = s0("w_nat", [P, 2, KC, D], F32)
        ends = s0("ends", [BP, 2, BC, EB], I32)
        part_i = s0("part_i", [BP, 4, BC, EB], I32)
        part_b = s0("part_b", [BP, 4, BC, EB], BF16)
        last_f = s0("last_f", [BP, BC], F32)
        d128 = s0("d128", [P, TILES], F32)
        d128_1 = s0("d128_1", [P, TILES], F32)
        before = s0("before", [BP, BC, TILES], BF16)
        first_b = s0("first_b", [P, TILES], F32)
        block_id = s0("block_id", [P, BC, WIN], F32)
        pick = s0("pick", [BP, WIN, BC, TILES], BF16)
        tmp = s0("tmp", [P, 5, TILES], F32)
        in_tile = s0("in_tile", [P, WIN, TILES], F32)
        member = s0("member", [P, WIN, TILES], BF16)
        covered = s0("covered", [P, 2], F32)
        left_f = s0("left_f", [P, 1], F32)
        part_no = s0("part_no", [P, 1], F32)
        row_i = s0("row_i", [P, 3, WIN, TILES], I32)
        e_src = s0("e_src", [P, 1], U32)
        e_dst = s0("e_dst", [P, 1], U32)
        e_row = s0("e_row", [P, P], U32)
        e_dst_f = s0("e_dst_f", [P, 1], F32)
        e_row_f = s0("e_row_f", [P, P], F32)
        same = s0("same", [P, P], F32)
        earlier = s0("earlier", [P, P], F32)
        repeated = s0("repeated", [P, 1], F32)
        e_write = s0("e_write", [P, 1], U32)
        e_x = s0("e_x", [P, CW], F32)
        e_sum = s0("e_sum", [P, CW], F32)
        e_count = s0("e_count", [P, 1], F32)
        zero.close()

        s1 = allocator(one)
        xs = s1("xs", [P, 2, GT, D], F32)
        hot_slot = s1("hot_slot", [P, 2, WIN, P], BF16)
        hot_dst = s1("hot_dst", [P, 2, WIN, P], BF16)
        ct = s1("ct", [P, 4, 8], F32)
        idx_u = s1("idx_u", [P, 4, 1], U32)
        spread = s1("spread", [P, 4, P], F32R)
        rows = s1("rows", [P, 2, D], F32)
        rows_hi = s1("rows_hi", [P, 2, D], F32R)
        rows_lo = s1("rows_lo", [P, 2, D], F32R)
        x_self = s1("x_self", [P, 2, D], F32)
        aggr = s1("aggr", [P, 2, D], F32)
        xT_hi = s1("xT_hi", [P, 2, KC, GR], F32R)
        xT_lo = s1("xT_lo", [P, 2, KC, GR], F32R)
        aT_hi = s1("aT_hi", [P, 2, KC, GR], F32R)
        aT_lo = s1("aT_lo", [P, 2, KC, GR], F32R)
        h_out = s1("h_out", [P, 2, KC, GR], F32)
        one.close()

        two = ExitStack()
        s2 = allocator(two)
        h2 = s2("h2", [P, H2, KC, GR], F32)
        x2 = s2("x2", [P, H2, GT, D], F32)
        r2 = s2("r2", [P, 2, KC, GR], F32)
        o2 = s2("o2", [P, 2, GT, D], F32)
        st2 = s2("st2", [P, 2, GT, 6], F32)
        mv2 = s2("mv2", [P, 2, GT, 2], F32)
        sd2 = s2("sd2", [P, 2, GT, 1], F32)
        rs2 = s2("rs2", [P, 2, GT, 1], F32)
        nm2 = s2("nm2", [P, 2, GT, 1], F32)
        two.close()

        ph = [ps(f"ph{i}", [P, GR]) for i in range(4)]
        pxT = ps("pxT", [P, KC, P])
        paT = ps("paT", [P, KC, P])
        pagg = ps("pagg", [P, D])
        pslot = ps("pslot", [P, 512])

        s_w = sem("w_loaded")
        s_ends = sem("ends_loaded")
        s_vec = sem("vec_loaded")
        s_const = sem("constants_ready")
        s_p0 = sem("prep_vector")
        s_pool0 = sem("pool_step")
        s_wT = sem("w_transposed")
        s_wh = sem("w_hi")
        s_wl = sem("w_lo")
        s_first = sem("first_blocks")
        s_win = sem("windows_picked")
        s_wu = sem("windows_read")
        s_rank = sem("ranks_summed")
        s_pv = sem("prep_vector_step")
        s_gv = sem("general_vector_step")
        s_tab = sem("tables_ready")
        s_cov = sem("covered_counted")
        s_covs = sem("covered_summed")
        s_flag = sem("left_over_ready")
        s_zero = sem("zeros_ready")
        s_zf = sem("sums_cleared")
        s_blk = sem("block_free")
        s_sl = sem("edges_loaded")
        s_eq = sem("same_row_steps")
        s_er = sem("repeats_found")
        s_sg = sem("sources_gathered")
        s_ss = sem("sums_gathered")
        s_sp = sem("block_summed")
        s_sa = sem("sums_added")
        s_sc = sem("sums_scattered")
        s_ml = sem("sums_loaded")
        s_mc = sem("mean_steps")
        s_mm = sem("means_ready")
        s_ms = sem("means_stored")
        s_mnext = sem("means_written")
        s_mdone = sem("general_path_done")
        s_x = [sem(f"x_loaded{b}") for b in range(2)]
        s_xp = sem("x_part_loaded")
        s_hot = sem("one_hots_built")
        s_comp = sem("slots_filled")
        s_is = sem("slot_steps")
        s_idx = sem("indices_ready")
        s_gat = [sem(f"rows_gathered{b}") for b in range(2)]
        s_go = sem("gather_allowed")
        s_gh = sem("rows_hi_ready")
        s_gl = sem("rows_lo_ready")
        s_agg = sem("rows_summed")
        s_xself = sem("x_self_ready")
        s_aggr = sem("aggr_ready")
        s_xtr = sem("x_transposed")
        s_xh = sem("xT_hi_ready")
        s_xl = sem("xT_lo_ready")
        s_atr = sem("aggr_transposed")
        s_ah = sem("aT_hi_ready")
        s_al = sem("aT_lo_ready")
        s_main = sem("h_summed")
        s_hc = sem("h_copied")
        s_bn = sem("h_counted")
        s_st = [sem(f"h_stored{b}") for b in range(2)]
        s_stfree = sem("h_out_free")
        s_mz = sem("moments_cleared")
        s_bnv = sem("bn_vector")
        s_bns = sem("bn_root")
        s_bnr = sem("bn_ready")
        s_h2 = [sem(f"h2_loaded{b}") for b in range(H2)]
        s_x2 = [sem(f"x2_loaded{b}") for b in range(H2)]
        s_x2p = sem("x2_part_loaded")
        s_relu = sem("relu_ready")
        s_t2 = sem("relu_transposed")
        s_y = sem("y_ready")
        s_m1 = sem("tile_counted")
        s_all = sem("group_counted")
        s_m2 = sem("moments_ready")
        s_sd = sem("deviation_ready")
        s_rs = sem("inverse_ready")
        s_oa = sem("normalised_by_act")
        s_od = sem("normalised_by_dve")
        s_os = [sem(f"out_stored{b}") for b in range(2)]

        block = ctx.enter_context(nc.Block())

        @block.sync
        def _(sp):
            sp.dma_start(ends[:, 0], src.rearrange("(c b p) -> b c p", b=BP, p=EB)).then_inc(s_ends, 16)
            sp.dma_start(ends[:, 1], dst.rearrange("(c b p) -> b c p", b=BP, p=EB)).then_inc(s_ends, 16)
            for m, w in enumerate((w_l, w_r)):
                sp.dma_start(w_nat[:, m], w.rearrange("(c f) k -> f c k", f=P)).then_inc(s_w, 16)
            with nc.allow_non_contiguous_dma(reason="three short vectors"):
                for m, v in enumerate((b_l, gamma, beta)):
                    sp.dma_start(vec[:, m], v.rearrange("(c p) -> p c", p=P)).then_inc(s_vec, 16)
            sp.wait_ge(s_flag, 1)
            with sp.If(sp.value_load(left_over[0:1, 0:1], min_val=0, max_val=E) > 0):
                sp.wait_ge(s_zero, 1)
                with sp.Fori(0, TILES - 1) as d:
                    sp.dma_start(sum_dram[bass.ds(d * P, P), :], e_sum[:]).then_inc(s_zf, 16)
                sp.dma_start(sum_dram[N - LAST_ROWS:N, :], e_sum[0:LAST_ROWS, :]).then_inc(s_zf, 16)
                sp.wait_ge(s_zf, 16 * TILES)
                sp.sem_inc(s_blk, 1)
                with sp.Fori(0, NB) as n:
                    sp.wait_ge(s_blk, n + 1)
                    with nc.allow_non_contiguous_dma(reason="an edge to a partition"):
                        for t, e in ((e_src, src), (e_dst, dst)):
                            sp.dma_start(t[0:EB, :], e.bitcast(U32)[bass.ds(n * EB, EB)]
                                         .rearrange("(p o) -> p o", o=1)).then_inc(s_sl, 16)
                    sp.dma_start(e_row[0:EB, 0:EB], dst.bitcast(U32)[bass.ds(n * EB, EB)]
                                 .rearrange("(o p) -> o p", o=1).to_broadcast([EB, EB])).then_inc(s_sl, 16)
                sp.wait_ge(s_blk, NB + 1)

                def mean_tile(d, n):
                    rows = bass.ds(d * P, n)
                    sp.dma_start(e_sum[0:n, :], sum_dram[rows, :]).then_inc(s_ml, 16)
                    sp.wait_ge(s_mm, d + 1)
                    sp.dma_start(mean_dram[rows, :], e_x[0:n, 0:D]).then_inc(s_ms, 16)
                    sp.wait_ge(s_ms, 16 * d + 16)
                    sp.sem_inc(s_mnext, 1)

                with sp.Fori(0, TILES - 1) as d:
                    mean_tile(d, P)
                mean_tile(TILES - 1, LAST_ROWS)
                sp.sem_inc(s_mdone, 1)
            sp.wait_ge(s_tab, 1)
            sp.wait_ge(s_wT, 2 * KC)

            def load_x(g, b):
                if isinstance(g, int) and (g + 1) * GR > N:
                    full = (N - g * GR) // P
                    lot = sp.dma_start(xs[:, b, 0:full],
                                       x[g * GR:g * GR + full * P, :].rearrange("(t p) f -> p t f", p=P))
                    lot.then_inc(s_x[b], 16)
                    sp.dma_start(xs[0:LAST_ROWS, b, full], x[N - LAST_ROWS:N, :]).then_inc(s_xp, 16)
                else:
                    sp.dma_start(xs[:, b], x_group(g)).then_inc(s_x[b], 16)

            def group(g, b, after):
                if after:
                    sp.wait_ge(s_xtr, GT * g + GT)
                    sp.wait_ge(s_xself, GT * g + GT)
                    load_x(g + 2, b)
                sp.wait_ge(s_hc, GT * g + 4 + GT)
                sp.dma_start(h_dram[g], h_out[:, b]).then_inc(s_st[b], 16)
                sp.wait_ge(s_st[b], 8 * (g - b) + 16)
                sp.sem_inc(s_stfree, 1)

            load_x(0, 0)
            load_x(1, 1)
            if PAIRS > 1:
                with sp.Fori(0, PAIRS - 1) as q:
                    for b in range(2):
                        group(2 * q + b, b, True)
            for g in range(2 * PAIRS - 2, GROUPS):
                group(g, g % 2, g + 2 < GROUPS)

            def load2(g, b):
                sp.dma_start(h2[:, b], h_dram[g]).then_inc(s_h2[b], 16)
                if isinstance(g, int) and (g + 1) * GR > N:
                    full = (N - g * GR) // P
                    sp.dma_start(x2[:, b, 0:full],
                                 x[g * GR:g * GR + full * P, :].rearrange("(t p) f -> p t f", p=P)).then_inc(s_x2[b], 16)
                    sp.dma_start(x2[0:LAST_ROWS, b, full], x[N - LAST_ROWS:N, :]).then_inc(s_x2p, 16)
                else:
                    sp.dma_start(x2[:, b], x_group(g)).then_inc(s_x2[b], 16)

            def store2(g, b):
                if isinstance(g, int) and (g + 1) * GR > N:
                    full = (N - g * GR) // P
                    sp.wait_ge(s_oa, 2 * g + 2)
                    sp.wait_ge(s_od, TILES - 2 * (g + 1))
                    sp.dma_start(out[g * GR:g * GR + full * P, :].rearrange("(t p) f -> p t f", p=P),
                                 o2[:, b, 0:full]).then_inc(s_os[b], 16)
                    sp.dma_start(out[N - LAST_ROWS:N, :], o2[0:LAST_ROWS, b, full]).then_inc(s_os[b], 16)
                else:
                    sp.wait_ge(s_oa, 2 * g + 2)
                    sp.wait_ge(s_od, 2 * g + 2)
                    sp.dma_start(out[bass.ds(g * GR, GR), :].rearrange("(t p) f -> p t f", p=P),
                                 o2[:, b]).then_inc(s_os[b], 16)

            sp.wait_ge(s_bnr, 1)
            for g in range(H2):
                load2(g, g)
            rounds2 = (GROUPS - 1 - H2) // H2
            if rounds2 > 0:
                with sp.Fori(0, rounds2) as q:
                    for k in range(H2):
                        store2(H2 * q + k, k % 2)
                        load2(H2 * q + (k + H2), k)
            for g in range(H2 * max(rounds2, 0), GROUPS):
                store2(g, g % 2)
                if g + H2 < GROUPS:
                    load2(g + H2, g % H2)
            for b in range(2):
                stores = len(range(b, GROUPS, 2)) + (b == (GROUPS - 1) % 2)
                sp.wait_ge(s_os[b], 16 * stores)

        @block.tensor
        def _(pe):
            pe.wait_ge(s_w, 32)
            pe.wait_ge(s_const, 1)
            for m in range(2):
                for kc in range(KC):
                    n = m * KC + kc
                    if n >= 4:
                        pe.wait_ge(s_wl, n - 3)
                    for fc in range(KC):
                        last = pe.transpose(ph[n % 4][:, fc * P:(fc + 1) * P],
                                            w_nat[:, m, fc, kc * P:(kc + 1) * P], ident[:])
                    last.then_inc(s_wT, 1)
            pe.wait_ge(s_p0, 1)
            for c in range(BC):
                last = pe.matmul(pslot[:, 0:TILES], ones_b[0:BP, :], before[:, c, :], start=c == 0, stop=c == BC - 1)
            last.then_inc(s_first, 1)
            for j in range(WIN):
                pe.wait_ge(s_p0, 2 + j)
                if j == 0:
                    pe.wait_ge(s_wl, 2 * KC)
                else:
                    pe.wait_ge(s_wu, j)
                for a in range(4):
                    for c in range(BC):
                        last = pe.matmul(ph[a][0:EB, 0:TILES], part_b[:, a, c, :], pick[:, j, c, :],
                                         start=c == 0, stop=c == BC - 1)
                last.then_inc(s_win, 1)
            pe.wait_ge(s_p0, 2 + WIN)
            for j in range(WIN):
                pe.matmul(ph[j][0:EB, 0:TILES], tri[0:EB, 0:EB], member[0:EB, j, :], start=True, stop=j == 0)
                for k in range(j):
                    last = pe.matmul(ph[j][0:EB, 0:TILES], ones_b[0:EB, 0:EB], member[0:EB, k, :], start=False, stop=k == j - 1)
            last.then_inc(s_rank, 1)
            pe.wait_ge(s_cov, 1)
            pe.matmul(pslot[0:1, 0:1], covered[0:EB, 0:1], ones_f[0:EB, :], start=True, stop=True).then_inc(s_covs, 1)
            pe.wait_ge(s_flag, 1)
            with pe.If(pe.value_load(left_over[0:1, 0:1], min_val=0, max_val=E) > 0):
                with pe.Fori(0, NB) as n:
                    pe.wait_ge(s_eq, 3 * n + 2)
                    pe.wait_ge(s_sg, 16 * n + 16)
                    pe.matmul(pagg[0:EB, :], same[0:EB, 0:EB], e_x[0:EB, 0:D], start=True, stop=True)
                    pe.matmul(pslot[0:EB, 0:CW - D], same[0:EB, 0:EB], e_x[0:EB, D:CW], start=True,
                              stop=True).then_inc(s_sp, 1)
            pe.wait_ge(s_tab, 1)

            def fill_slots(base, c):
                i = base + c
                b = c % 2
                pe.wait_ge(s_hot, i + 1)
                if not (isinstance(i, int) and i == 0):
                    pe.wait_ge(s_is, 4 * i - 3)
                for j in range(WIN):
                    pe.matmul(pslot[:, 0:3], hot_slot[0:EB, b, j, :], vals[0:EB, j, i, 0:3],
                              start=j == 0, stop=j == WIN - 1)
                for j in range(WIN):
                    last = pe.matmul(pslot[:, 3:5], hot_dst[0:EB, b, j, :], vals[0:EB, j, i, 3:5],
                                     start=j == 0, stop=j == WIN - 1)
                last.then_inc(s_comp, 1)

            def sum_rows(base, c):
                i = base + c
                b = c % 2
                pe.wait_ge(s_gl, i + 1)
                pe.wait_ge(s_idx, i + 1)
                if not (isinstance(i, int) and i == 0):
                    pe.wait_ge(s_aggr, i)
                pe.matmul(pagg[:], spread[:, c % 4, :], rows_hi[:, b, :], start=True, stop=False)
                pe.matmul(pagg[:], spread[:, c % 4, :], rows_lo[:, b, :], start=False, stop=True).then_inc(s_agg, 1)

            def transpose_x(base, c):
                i = base + c
                b, t, n = c // GT % 2, c % GT, rows_of(i)
                pe.wait_ge(s_x[b], 2 * base + 16 * (c // LOOP) + 16)
                if n < P:
                    pe.wait_ge(s_xp, 16)
                if not (isinstance(i, int) and i == 0):
                    pe.wait_ge(s_xl, i)
                for kc in range(KC):
                    last = pe.transpose(pxT[:, kc, 0:n], xs[0:n, b, t, kc * P:(kc + 1) * P], ident[0:n, 0:n])
                last.then_inc(s_xtr, 1)

            def transpose_aggr(base, c):
                i = base + c
                n = rows_of(i)
                pe.wait_ge(s_aggr, i + 1)
                if not (isinstance(i, int) and i == 0):
                    pe.wait_ge(s_al, i)
                for kc in range(KC):
                    last = pe.transpose(paT[:, kc, 0:n], aggr[0:n, c % 2, kc * P:(kc + 1) * P], ident[0:n, 0:n])
                last.then_inc(s_atr, 1)

            def product(base, c, m, hi, lo, first):
                b, fc = c // GT % 2, c % GT
                u = base + c
                cols = GR
                if isinstance(base, int):
                    cols = min(GR, N - (u // GT) * GR)
                for kc in range(KC):
                    for part, side in (("hi", hi), ("hi", lo), ("lo", hi)):
                        done = not first and kc == KC - 1 and part == "lo"
                        last = pe.matmul(ph[fc][:, 0:cols], wT[m, part][:, kc, fc * P:(fc + 1) * P],
                                         side[:, b, kc, 0:cols],
                                         start=first and kc == 0 and part == "hi" and side is hi, stop=done)
                return last

            def slot(base, c, main):
                if exists(base + c + 7):
                    fill_slots(base, c + 7)
                if exists(base + c + 5):
                    sum_rows(base, c + 5)
                if exists(base + c + 4):
                    transpose_x(base, c + 4)
                u = base + c
                ready = GT * (c // GT) + GT + base
                if isinstance(ready, int):
                    ready = min(ready, TILES)
                if main:
                    pe.wait_ge(s_hc, u + 1)
                    if c % GT == 0:
                        pe.wait_ge(s_xl, ready)
                    product(base, c, "r", xT_hi, xT_lo, True)
                if exists(base + c + 4):
                    transpose_aggr(base, c + 4)
                if main:
                    if c % GT == 0:
                        pe.wait_ge(s_al, ready)
                    product(base, c, "l", aT_hi, aT_lo, False).then_inc(s_main, 1)

            for c in range(-8, 0):
                slot(0, c, False)
            with pe.Fori(0, PAIRS) as q:
                for c in range(LOOP):
                    slot(LOOP * q, c, True)
            for c in range(GROUPS * GT - REST):
                slot(REST, c, True)

            def back(g, b, cols):
                for t in range(-(-cols // P)):
                    n = min(P, cols - t * P)
                    if t == 0:
                        pe.wait_ge(s_relu, GT * g + GT)
                    if not isinstance(g, int) or g > 0:
                        pe.wait_ge(s_y, GT * g + t - 3)
                    for fc in range(KC):
                        last = pe.transpose(ph[t][0:n, fc * P:(fc + 1) * P], r2[:, b, fc, t * P:t * P + n], ident[:])
                    last.then_inc(s_t2, 1)

            for g in range(2):
                back(g, g, GR)
            with pe.Fori(1, PAIRS) as q:
                for b in range(2):
                    back(2 * q + b, b, GR)
            for g in range(2 * PAIRS, GROUPS):
                back(g, g % 2, min(GR, N - g * GR))

        @block.scalar
        def _(act):
            for n in range(2 * KC):
                act.wait_ge(s_wT, n + 1)
                act.activation(wT["lr"[n // KC], "hi"][:, n % KC, :], ph[n % 4][:], ACT.Copy).then_inc(s_wh, 1)
            act.sem_inc(s_hc, 4)
            act.sem_inc(s_stfree, 2)
            act.wait_ge(s_tab, 1)
            act.wait_ge(s_vec, 48)

            def self_share(base, c):
                i = base + c
                b, t, n = c // GT % 2, c % GT, rows_of(i)
                act.wait_ge(s_x[b], 2 * base + 16 * (c // LOOP) + 16)
                if n < P:
                    act.wait_ge(s_xp, 16)
                act.wait_ge(s_is, 4 * i + 4)
                if not (isinstance(i, int) and i < 2):
                    act.wait_ge(s_aggr, i - 1)
                act.activation(x_self[0:n, c % 2, :], xs[0:n, b, t, :], ACT.Copy,
                               scale=ct[0:n, c % 4, 7:8]).then_inc(s_xself, 1)

            def hi_of(base, c, bank, ready, side, done):
                i = base + c
                b, t, n = c // GT % 2, c % GT, rows_of(i)
                act.wait_ge(ready, i + 1)
                if not (isinstance(i, int) and i < LOOP):
                    act.wait_ge(s_main, GT * (c // GT) + base - GT)
                act.activation(side[:, b, :, t * P:t * P + n], bank[:, :, 0:n], ACT.Copy).then_inc(done, 1)

            def rows_high(base, c):
                i = base + c
                if isinstance(i, int):
                    act.wait_ge(s_gat[c % 2], 16 * (i // 2 + 1))
                else:
                    act.wait_ge(s_gat[c % 2], 8 * base + 16 * (c // 2 + 1))
                if not (isinstance(i, int) and i < 2):
                    act.wait_ge(s_agg, i - 1)
                act.activation(rows_hi[:, c % 2, :], rows[:, c % 2, :], ACT.Copy).then_inc(s_gh, 1)

            def copy_h(base, c):
                u = base + c
                b, fc = c // GT % 2, c % GT
                cols = min(GR, N - (u // GT) * GR) if isinstance(base, int) else GR
                act.wait_ge(s_main, u + 1)
                if fc == 0:
                    g1 = c // GT + (base // GT if isinstance(base, int) else q2[0])
                    act.wait_ge(s_stfree, g1 + 1)
                    act.wait_ge(s_bn, GT * g1 + GT)
                act.activation(h_out[:, b, fc, 0:cols], ph[fc][:, 0:cols], ACT.Identity,
                               bias=vec[:, 0, fc:fc + 1]).then_inc(s_hc, 1)

            q2 = [0]

            def slot(base, c, main):
                if exists(base + c + 5):
                    self_share(base, c + 5)
                if exists(base + c + 4):
                    hi_of(base, c + 4, pxT, s_xtr, xT_hi, s_xh)
                    hi_of(base, c + 4, paT, s_atr, aT_hi, s_ah)
                if exists(base + c + 6):
                    rows_high(base, c + 6)
                if main:
                    copy_h(base, c)

            for c in range(-8, 0):
                slot(0, c, False)
            with act.Fori(0, PAIRS) as q:
                q2[0] = 2 * q
                for c in range(LOOP):
                    slot(LOOP * q, c, True)
            for c in range(GROUPS * GT - REST):
                slot(REST, c, True)

            act.wait_ge(s_bnv, 1)
            act.activation(bn_t[:, 0, :], bn_mv[:, :, 1], ACT.Sqrt, bias=eps_c[:]).then_inc(s_bns, 1)
            act.wait_ge(s_bnr, 1)

            def relu(g, k, loaded, cols):
                b = k % 2
                act.wait_ge(s_h2[k % H2], loaded)
                if not isinstance(g, int) or g >= 2:
                    act.wait_ge(s_t2, GT * g - GT)
                for fc in range(KC):
                    act.activation(r2[:, b, fc, 0:cols], h2[:, k % H2, fc, 0:cols], ACT.Relu,
                                   bias=bn_bias[:, fc:fc + 1], scale=bn_scale[:, fc:fc + 1]).then_inc(s_relu, 1)

            def root(g, k):
                b = k % 2
                act.wait_ge(s_m2, GT * g + GT)
                act.activation(sd2[:, b, :, 0], mv2[:, b, :, 1], ACT.Sqrt, bias=eps_c[:]).then_inc(s_sd, 1)

            def normalise(g, k):
                b = k % 2
                act.wait_ge(s_rs, 2 * g + 2)
                if not isinstance(g, int) or g >= 2:
                    act.wait_ge(s_os[b], 8 * (g - b))
                for t in range(2):
                    act.activation(o2[:, b, t, :], x2[:, k % H2, t, :], ACT.Identity, bias=nm2[:, b, t, :],
                                   scale=rs2[:, b, t, :]).then_inc(s_oa, 1)

            def step2(g, k, loaded):
                if not isinstance(g, int) or g + 1 < GROUPS:
                    relu(g + 1, k + 1, loaded, min(GR, N - (g + 1) * GR) if isinstance(g, int) else GR)
                if not isinstance(g, int) or g > 0:
                    normalise(g - 1, k - 1)
                if not isinstance(g, int) or g < GROUPS:
                    root(g, k)

            relu(0, 0, 16, GR)
            for g in range(H2):
                step2(g, g, 16 * ((g + 1) // H2) + 16)
            if ROUNDS2 > 1:
                with act.Fori(1, ROUNDS2) as q:
                    for k in range(H2):
                        step2(H2 * q + k, k, 16 * q + 16 * ((k + 1) // H2) + 16)
            for g in range(H2 * max(ROUNDS2, 1), GROUPS + 1):
                step2(g, g, 16 * ((g + 1) // H2) + 16)

        @block.vector
        def _(dve):
            steps = {s_pv: 0, s_gv: 0}

            def link(ins, s=s_pv):
                steps[s] += 1
                ins.then_inc(s, 1)
                dve.wait_ge(s, steps[s])

            dve.memset(eps_c[:], EPS)
            dve.memset(vals[:, :, :, 3:4], 1.0)
            dve.memset(ones_f[:], 1.0)
            dve.wait_ge(s_ends, 32)
            dve.wait_ge(s_const, 2)
            dve.tensor_copy(last_f[:], ends[:, 1, :, EB - 1])
            link(dve.tensor_scalar(part_i[:, 0], ends[:, 1], 1, None, ALU.add))
            link(dve.tensor_scalar(part_i[:, 2], part_i[:, 0], 8, None, ALU.logical_shift_right))
            link(dve.tensor_scalar(part_i[:, 3], part_i[:, 0], 255, None, ALU.bitwise_and))
            link(dve.tensor_scalar(part_i[:, 0], ends[:, 0], 8, None, ALU.logical_shift_right))
            link(dve.tensor_scalar(part_i[:, 1], ends[:, 0], 255, None, ALU.bitwise_and))
            link(dve.tensor_copy(part_b[:], part_i[:]))
            for c in range(BC):
                last = dve.tensor_scalar(before[:, c, :], d128[0:BP, :], last_f[:, c:c + 1], None, ALU.is_gt)
            last.then_inc(s_p0, 1)
            for n in range(2 * KC):
                dve.wait_ge(s_wh, n + 1)
                w = "lr"[n // KC]
                dve.tensor_tensor(wT[w, "lo"][:, n % KC, :], ph[n % 4][:], wT[w, "hi"][:, n % KC, :].bitcast(F32),
                                  ALU.subtract).then_inc(s_wl, 1)
            dve.wait_ge(s_first, 1)
            link(dve.tensor_copy(first_b[:], pslot[:, 0:TILES]))
            for j in range(WIN):
                for c in range(BC):
                    last = dve.tensor_scalar(pick[:, j, c, :], first_b[0:BP, :], block_id[0:BP, c, j:j + 1], None,
                                             ALU.is_equal)
                last.then_inc(s_p0, 1)
            a = slice(0, EB)
            for j in range(WIN):
                dve.wait_ge(s_win, j + 1)
                sh, slo, dh, dlo = (ph[k][a, 0:TILES] for k in range(4))
                dve.tensor_scalar(vals[a, j, 0:TILES, 0], sh, 256.0, None, ALU.subtract)
                dve.tensor_copy(vals[a, j, 0:TILES, 1], slo)
                dve.tensor_copy(tmp[a, 1], dlo)
                link(dve.tensor_scalar(tmp[a, 0], slo, 1.0, None, ALU.add))
                dve.scalar_tensor_tensor(tmp[a, 2], sh, 256.0, tmp[a, 0], ALU.mult, ALU.add)
                dve.scalar_tensor_tensor(tmp[a, 3], dh, 256.0, tmp[a, 1], ALU.mult, ALU.add).then_inc(s_wu, 1)
                dve.wait_ge(s_wu, j + 1)
                link(dve.tensor_tensor(tmp[a, 4], tmp[a, 2], tmp[a, 3], ALU.is_equal))
                dve.tensor_copy(vals[a, j, 0:TILES, 4], tmp[a, 4])
                link(dve.tensor_tensor(dl[a, j, 0:TILES], tmp[a, 3], d128_1[a, :], ALU.subtract))
                link(dve.tensor_scalar(tmp[a, 0], dl[a, j, 0:TILES], 0.0, None, ALU.is_ge))
                link(dve.scalar_tensor_tensor(in_tile[a, j, :], dl[a, j, 0:TILES], float(P), tmp[a, 0], ALU.is_lt, ALU.mult))
                dve.tensor_scalar(vals[a, j, 0:TILES, 2], dl[a, j, 0:TILES], float(P), None, ALU.subtract)
                last = dve.scalar_tensor_tensor(member[a, j, :], tmp[a, 4], 0.5, in_tile[a, j, :], ALU.is_lt, ALU.mult)
            last.then_inc(s_p0, 1)
            dve.wait_ge(s_rank, 1)
            for j in range(WIN):
                last = dve.scalar_tensor_tensor(slot1[a, j, 0:TILES], ph[j][a, 0:TILES], 1.0, member[a, j, :],
                                                ALU.add, ALU.mult)
            link(last)
            link(dve.tensor_reduce(covered[a, 0:1], in_tile[a], AX.XY, ALU.add))
            link(dve.tensor_scalar(in_tile[a], slot1[a, :, 0:TILES], float(P), None, ALU.is_gt))
            link(dve.tensor_reduce(covered[a, 1:2], in_tile[a], AX.XY, ALU.add))
            dve.tensor_tensor(covered[a, 0:1], covered[a, 0:1], covered[a, 1:2], ALU.subtract).then_inc(s_cov, 1)
            dve.wait_ge(s_covs, 1)
            link(dve.tensor_scalar(left_f[0:1, :], pslot[0:1, 0:1], -1.0, float(E), ALU.mult, ALU.add))
            dve.tensor_copy(left_over[0:1, :], left_f[0:1, :]).then_inc(s_flag, 1)
            dve.wait_ge(s_flag, 1)
            with dve.If(dve.value_load(left_over[0:1, 0:1], min_val=0, max_val=E) > 0):
                link(dve.memset(e_x[:], 1.0), s_gv)
                dve.memset(e_sum[:], 0.0).then_inc(s_zero, 1)
                with dve.Fori(0, NB) as n:
                    dve.wait_ge(s_sl, 48 * n + 48)
                    dve.tensor_copy(e_row_f[a, 0:EB], e_row[a, 0:EB])
                    dve.tensor_copy(e_dst_f[a], e_dst[a]).then_inc(s_eq, 1)
                    dve.wait_ge(s_eq, 3 * n + 1)
                    dve.tensor_scalar(same[a, 0:EB], e_row_f[a, 0:EB], e_dst_f[a], None, ALU.is_equal).then_inc(s_eq, 1)
                    dve.wait_ge(s_eq, 3 * n + 2)
                    dve.scalar_tensor_tensor(earlier[a, 0:EB], iota_0[a, 0:EB], part_no[a], same[a, 0:EB],
                                             ALU.is_lt, ALU.mult).then_inc(s_eq, 1)
                    dve.wait_ge(s_eq, 3 * n + 3)
                    dve.tensor_reduce(repeated[a], earlier[a, 0:EB], AX.X, ALU.max).then_inc(s_er, 1)
                    dve.wait_ge(s_er, n + 1)
                    dve.scalar_tensor_tensor(e_write[a], repeated[a], float(EMPTY), e_dst_f[a], ALU.mult, ALU.add)
                    dve.wait_ge(s_sp, n + 1)
                    dve.wait_ge(s_ss, 16 * n + 16)
                    dve.tensor_tensor(e_sum[a, 0:D], pagg[a, :], e_sum[a, 0:D], ALU.add)
                    dve.tensor_tensor(e_sum[a, D:CW], pslot[a, 0:CW - D], e_sum[a, D:CW], ALU.add).then_inc(s_sa, 1)

                def mean_tile(d, n):
                    dve.wait_ge(s_ml, 16 * d + 16)
                    dve.tensor_scalar(e_count[0:n], e_sum[0:n, D:D + 1], 1.0, None, ALU.max).then_inc(s_mc, 1)
                    dve.wait_ge(s_mc, 2 * d + 1)
                    dve.reciprocal(e_count[0:n], e_count[0:n]).then_inc(s_mc, 1)
                    dve.wait_ge(s_mc, 2 * d + 2)
                    dve.tensor_scalar(e_x[0:n, 0:D], e_sum[0:n, 0:D], e_count[0:n], None, ALU.mult).then_inc(s_mm, 1)

                with dve.Fori(0, TILES - 1) as d:
                    mean_tile(d, P)
                mean_tile(TILES - 1, LAST_ROWS)
                dve.wait_ge(s_mdone, 1)
                dve.tensor_scalar(row_i[a, 1], row_i[a, 0], 8, None, ALU.logical_shift_right)
                link(dve.tensor_scalar(row_i[a, 2], row_i[a, 0], 255, None, ALU.bitwise_and), s_gv)
                for j in range(WIN):
                    dve.tensor_scalar(vals[a, j, 0:TILES, 0], row_i[a, 1, j], 256.0, None, ALU.subtract)
                    dve.tensor_copy(vals[a, j, 0:TILES, 1], row_i[a, 2, j])
                    link(dve.tensor_copy(in_tile[a, j], row_i[a, 0, j]), s_gv)
                    link(dve.tensor_tensor(dl[a, j, 0:TILES], in_tile[a, j], d128[a, :], ALU.subtract), s_gv)
                    dve.tensor_scalar(vals[a, j, 0:TILES, 2], dl[a, j, 0:TILES], float(P), None, ALU.subtract)
                    dve.tensor_scalar(slot1[a, j, 0:TILES], dl[a, j, 0:TILES], 1.0, None, ALU.add)
                link(dve.memset(vals[:, :, :, 4:5], 0.0), s_gv)
            dve.memset(slot1[:, :, TILES:TILES + 1], 0.0)
            dve.memset(dl[:, :, TILES:TILES + 1], -1.0).then_inc(s_tab, 1)
            dve.sem_inc(s_bn, 8)
            dve.wait_ge(s_tab, 1)

            def one_hots(base, c):
                i = base + c
                b = c % 2
                if not (isinstance(i, int) and i < 2):
                    dve.wait_ge(s_comp, i - 1)
                for j in range(WIN):
                    dve.tensor_scalar(hot_slot[a, b, j, :], iota_1[a, :], slot1[a, j, bass.ds(i, 1)], None, ALU.is_equal)
                for j in range(WIN):
                    last = dve.tensor_scalar(hot_dst[a, b, j, :], iota_0[a, :], dl[a, j, bass.ds(i, 1)], None, ALU.is_equal)
                last.then_inc(s_hot, 1)

            def indices(base, c):
                i = base + c
                k = c % 4
                dve.wait_ge(s_comp, i + 1)
                dve.tensor_copy(ct[:, k, 0:5], pslot[:, 0:5]).then_inc(s_is, 1)
                dve.wait_ge(s_is, 4 * i + 1)
                dve.scalar_tensor_tensor(ct[:, k, 5:6], ct[:, k, 0:1], 256.0, ct[:, k, 1:2], ALU.mult, ALU.add)
                dve.tensor_scalar(ct[:, k, 6:7], ct[:, k, 3:4], 1.0, None, ALU.max).then_inc(s_is, 1)
                dve.wait_ge(s_is, 4 * i + 2)
                dve.tensor_scalar(idx_u[:, k, :], ct[:, k, 5:6], float(EMPTY), None, ALU.add)
                dve.reciprocal(ct[:, k, 6:7], ct[:, k, 6:7]).then_inc(s_is, 1)
                dve.tensor_scalar(spread[:, k, :], iota_m[:], ct[:, k, 2:3], None, ALU.is_equal).then_inc(s_idx, 1)
                dve.wait_ge(s_is, 4 * i + 3)
                dve.tensor_tensor(ct[:, k, 7:8], ct[:, k, 4:5], ct[:, k, 6:7], ALU.mult).then_inc(s_is, 1)

            def mean(base, c):
                i = base + c
                n = rows_of(i)
                dve.wait_ge(s_agg, i + 1)
                dve.wait_ge(s_xself, i + 1)
                if not (isinstance(i, int) and i < 2):
                    dve.wait_ge(s_atr, i - 1)
                dve.scalar_tensor_tensor(aggr[0:n, c % 2, :], pagg[0:n, :], ct[0:n, c % 4, 6:7], x_self[0:n, c % 2, :],
                                         ALU.mult, ALU.add).then_inc(s_aggr, 1)

            def lo_of(base, c, bank, ready, hi, lo, done):
                i = base + c
                b, t, n = c // GT % 2, c % GT, rows_of(i)
                dve.wait_ge(ready, i + 1)
                dve.tensor_tensor(lo[:, b, :, t * P:t * P + n], bank[:, :, 0:n],
                                  hi[:, b, :, t * P:t * P + n].bitcast(F32), ALU.subtract).then_inc(done, 1)

            def count_h(base, c):
                u = base + c
                fc = c % GT
                cols = min(GR, N - (u // GT) * GR) if isinstance(base, int) else GR
                g = c // GT + (base // GT if isinstance(base, int) else q2[0])
                dve.wait_ge(s_hc, u + 5)
                dve.bn_stats(stats[:, fc, g, :], h_out[:, c // GT % 2, fc, 0:cols]).then_inc(s_bn, 1)

            q2 = [0]

            def slot(base, c, main):
                if exists(base + c + 7):
                    indices(base, c + 7)
                if exists(base + c + 5):
                    mean(base, c + 5)
                if exists(base + c + 8):
                    one_hots(base, c + 8)
                if exists(base + c + 4):
                    lo_of(base, c + 4, pxT, s_xh, xT_hi, xT_lo, s_xl)
                    lo_of(base, c + 4, paT, s_ah, aT_hi, aT_lo, s_al)
                if main:
                    count_h(base, c)

            for c in range(-8, 0):
                slot(0, c, False)
            with dve.Fori(0, PAIRS) as q:
                q2[0] = 2 * q
                for c in range(LOOP):
                    slot(LOOP * q, c, True)
            for c in range(GROUPS * GT - REST):
                slot(REST, c, True)

            dve.wait_ge(s_bn, GROUPS * GT + 8)
            dve.wait_ge(s_vec, 48)
            for fc in range(KC):
                last = dve.bn_aggr(bn_mv[:, fc, :], stats[:, fc].rearrange("p g s -> p (g s)"))
            last.then_inc(s_bnv, 1)
            dve.wait_ge(s_bns, 1)
            link(dve.reciprocal(bn_t[:, 1, :], bn_t[:, 0, :]))
            link(dve.tensor_tensor(bn_scale[:], bn_t[:, 1, :], vec[:, 1, :], ALU.mult))
            link(dve.tensor_tensor(bn_t[:, 2, :], bn_mv[:, :, 0], bn_scale[:], ALU.mult))
            dve.tensor_tensor(bn_bias[:], vec[:, 2, :], bn_t[:, 2, :], ALU.subtract).then_inc(s_bnr, 1)

            def sum_y(g, k, loaded, cols):
                b, tiles = k % 2, -(-cols // P)
                for t in range(tiles):
                    n = min(P, cols - t * P)
                    dve.wait_ge(s_t2, GT * g + t + 1)
                    if t == 0:
                        dve.wait_ge(s_x2[k % H2], loaded)
                    if n < P:
                        dve.wait_ge(s_x2p, 16)
                    dve.tensor_tensor(x2[0:n, k % H2, t, :], ph[t][0:n, :], x2[0:n, k % H2, t, :],
                                      ALU.add).then_inc(s_y, 1)
                if not isinstance(g, int) or g >= 2:
                    dve.wait_ge(s_oa, 2 * g - 2)
                for t in range(tiles):
                    n = min(P, cols - t * P)
                    dve.wait_ge(s_y, GT * g + t + 1)
                    dve.bn_stats(st2[0:n, b, t, :], x2[0:n, k % H2, t, :]).then_inc(s_m1, 1)
                dve.wait_ge(s_m1, GT * g + tiles)
                dve.sem_inc(s_all, 1)
                for t in range(tiles):
                    n = min(P, cols - t * P)
                    last = dve.bn_aggr(mv2[0:n, b, t, :], st2[0:n, b, t, :])
                    last.then_inc(s_m2, 1 if t < tiles - 1 else GT - tiles + 1)

            def invert(g, k):
                b = k % 2
                dve.wait_ge(s_sd, g + 1)
                dve.reciprocal(rs2[:, b], sd2[:, b]).then_inc(s_rs, 1)
                dve.wait_ge(s_rs, 2 * g + 1)
                dve.scalar_tensor_tensor(nm2[:, b, :, 0], mv2[:, b, :, 0], -1.0, rs2[:, b, :, 0],
                                         ALU.mult, ALU.mult).then_inc(s_rs, 1)

            def normalise(g, k):
                b = k % 2
                dve.wait_ge(s_rs, 2 * g + 2)
                if not isinstance(g, int) or g >= 2:
                    dve.wait_ge(s_os[b], 8 * (g - b))
                for t in range(2, GT):
                    n = min(P, N - g * GR - t * P) if isinstance(g, int) else P
                    if n > 0:
                        dve.tensor_scalar(o2[0:n, b, t, :], x2[0:n, k % H2, t, :], mv2[0:n, b, t, 0:1],
                                          rs2[0:n, b, t, :], ALU.subtract, ALU.mult).then_inc(s_od, 1)

            def step2(g, k, loaded):
                if not isinstance(g, int) or g < GROUPS:
                    sum_y(g, k, loaded, min(GR, N - g * GR) if isinstance(g, int) else GR)
                if not isinstance(g, int) or g > 0:
                    normalise(g - 1, k - 1)
                if not isinstance(g, int) or g < GROUPS:
                    invert(g, k)

            dve.memset(mv2[:], 1.0).then_inc(s_mz, 1)
            dve.wait_ge(s_mz, 1)
            for g in range(H2):
                step2(g, g, 16)
            if ROUNDS2 > 1:
                with dve.Fori(1, ROUNDS2) as q:
                    for k in range(H2):
                        step2(H2 * q + k, k, 16 * q + 16)
            for g in range(H2 * max(ROUNDS2, 1), GROUPS + 1):
                step2(g, g, 16 * (g // H2) + 16)

        @block.gpsimd
        def _(pool):
            def number(t, pattern, base, channel):
                return pool.iota(t, pattern, base=base, channel_multiplier=channel, allow_small_or_imprecise_dtypes=True)

            pool.memset(ident[:], 0.0)
            pool.memset(tri[:], 1.0)
            pool.memset(ones_b[:], 1.0).then_inc(s_pool0, 1)
            pool.wait_ge(s_pool0, 1)
            pool.affine_select(out=ident[:], in_=ident[:], compare_op=ALU.not_equal, fill=1.0, base=0,
                               pattern=[[-1, P]], channel_multiplier=1).then_inc(s_const, 1)
            pool.affine_select(out=tri[:], in_=tri[:], compare_op=ALU.is_gt, fill=0.0, base=0,
                               pattern=[[1, P]], channel_multiplier=-1)
            number(d128[:], [[P, TILES]], 0, 0)
            number(d128_1[:], [[P, TILES]], 1, 0)
            number(block_id[:], [[BP, BC], [-1, WIN]], 0, 1)
            number(row_i[:, 0], [[EB, WIN], [P, TILES]], 0, 1)
            number(part_no[:], [[0, 1]], 0, 1)
            number(iota_m[:], [[1, P]], -P, 0)
            number(iota_0[:], [[1, P]], 0, 0)
            number(iota_1[:], [[1, P]], 1, 0).then_inc(s_const, 1)
            pool.wait_ge(s_flag, 1)
            left = pool.value_load(left_over[0:1, 0:1], min_val=0, max_val=E)

            def indexed(out, table, of, index, scatter=False):
                by = bass.IndirectOffsetOnAxis(ap=index, axis=0)
                return pool.indirect_dma_start(out=table if scatter else out, out_offset=by if scatter else None,
                                               in_=out if scatter else table, in_offset=None if scatter else by,
                                               bounds_check=of - 1, oob_is_err=False)

            with pool.If(left > 0):
                pool.wait_ge(s_zf, 16 * TILES)
                with pool.Fori(0, NB) as n:
                    pool.wait_ge(s_sl, 48 * n + 48)
                    pool.sem_inc(s_go, 1)
                    indexed(e_x[0:EB, 0:D], x[:, :], N, e_src[0:EB, :]).then_inc(s_sg, 16)
                    indexed(e_sum[0:EB, :], sum_dram[:, :], N, e_dst[0:EB, :]).then_inc(s_ss, 16)
                    pool.wait_ge(s_sa, n + 1)
                    pool.sem_inc(s_go, 1)
                    indexed(e_sum[0:EB, :], sum_dram[:, :], N, e_write[0:EB, :], scatter=True).then_inc(s_sc, 16)
                    pool.wait_ge(s_sc, 16 * n + 16)
                    pool.sem_inc(s_blk, 1)
            pool.wait_ge(s_tab, 1)
            pool.memset(rows[:], 0.0).then_inc(s_pool0, 1)
            pool.wait_ge(s_pool0, 2)

            last_row = pool.alloc_register("last_row")
            pool.reg_mov(last_row, N - 1)

            def gather(base, c):
                i = base + c
                pool.wait_ge(s_idx, i + 1)
                if not (isinstance(i, int) and i < 2):
                    pool.wait_ge(s_gl, i - 1)
                pool.sem_inc(s_go, 1)
                with pool.If(left > 0):
                    indexed(rows[:, c % 2, :], mean_dram[:, :], N, idx_u[:, c % 4, :]).then_inc(s_gat[c % 2], 16)
                with pool.Else():
                    indexed(rows[:, c % 2, :], x[:, :], N, idx_u[:, c % 4, :]).then_inc(s_gat[c % 2], 16)

            def rows_low(base, c):
                i = base + c
                pool.wait_ge(s_gh, i + 1)
                pool.tensor_tensor(rows_lo[:, c % 2, :], rows[:, c % 2, :], rows_hi[:, c % 2, :].bitcast(F32),
                                   ALU.subtract).then_inc(s_gl, 1)

            def slot(base, c):
                if exists(base + c + 7):
                    gather(base, c + 7)
                if exists(base + c + 6):
                    rows_low(base, c + 6)

            for c in range(-8, 0):
                slot(0, c)
            with pool.Fori(0, PAIRS) as q:
                for c in range(LOOP):
                    slot(LOOP * q, c)
            for c in range(TILES - REST):
                slot(REST, c)


_INS = ["x", "src", "dst", "L0_gnn_W_l", "L0_gnn_b_l", "L0_gnn_W_r", "L0_gnn_gamma", "L0_gnn_beta"]


def kernel(**inputs):
    import numpy as np
    import concourse.bacc as bacc
    from concourse.bass_utils import run_bass_kernel_spmd

    nc = bacc.Bacc("TRN2", target_bir_lowering=False, num_devices=1)
    arrays, args = {}, []
    for name in _INS:
        a = np.ascontiguousarray(inputs[name])
        arrays[name] = a
        args.append(nc.dram_tensor(name, a.shape, mybir.dt.from_np(a.dtype), kind="ExternalInput").ap())
    out = nc.dram_tensor("out", arrays["x"].shape, F32, kind="ExternalOutput").ap()
    bass_sage_batchnorm_residual_layernorm_kernel(nc, *args, out)
    return run_bass_kernel_spmd(nc, [arrays], core_ids=[0]).results[0]["out"]
```

```python
from contextlib import ExitStack

import concourse.bass as bass
from concourse import mybir

ALU = mybir.AluOpType
ACT = mybir.ActivationFunctionType
AX = mybir.AxisListType
F32 = mybir.dt.float32
F32R = mybir.dt.float32r
BF16 = mybir.dt.bfloat16
I32 = mybir.dt.int32
U32 = mybir.dt.uint32

P = 128
GT = 4
GR = GT * P
WIN = 3
LOOP = 2 * GT
H2 = 4
EPS = 1e-5


def largest_divisor(n, most):
    return max(k for k in range(1, most + 1) if n % k == 0)


def bass_sage_batchnorm_residual_layernorm_kernel(
    nc, x, xT_whole, xT_part, src, dst, wT_l, b_l, wT_r, gamma, beta, out
):
    N, D = x.shape
    E = src.shape[0]
    KC = D // P
    TILES = -(-N // P)
    GROUPS = -(-TILES // GT)
    LAST_ROWS = N - (TILES - 1) * P
    EB = largest_divisor(E, P)
    NB = E // EB
    BP = largest_divisor(NB, P)
    BC = NB // BP
    PAIRS = (GROUPS - 1) // 2
    ROUNDS2 = (GROUPS - 1) // H2
    REST = LOOP * PAIRS
    EMPTY = 1 << 16
    assert D == KC * P and KC == GT and N < EMPTY and TILES <= 512
    assert WIN * EB >= P
    assert REST + 7 >= TILES and REST + LOOP >= GROUPS * GT - GT + 1 and PAIRS >= 1

    def rows_of(i):
        return LAST_ROWS if isinstance(i, int) and i == TILES - 1 else P

    def chunk_exists(i):
        return not isinstance(i, int) or i < GROUPS * GT

    def x_chunks(base, c):
        first = c - c % GT + GT
        chunks = ((0,), (1,), (2, 3), ())[c % GT]
        return [first + k for k in chunks if chunk_exists(base + first) and not (
            isinstance(base, int) and base + first < GT)]

    def exists(i):
        return not isinstance(i, int) or 0 <= i < TILES

    CW = D + 8
    sum_dram = nc.dram_tensor("sum_scratch", (N, CW), F32).ap()
    mean_dram = nc.dram_tensor("mean_scratch", (N, D), F32).ap()
    h_dram = nc.dram_tensor("h_scratch", (GROUPS, P, KC, GR), F32).ap()

    def x_group(g):
        return x[bass.ds(g * GR, GR), :].rearrange("(t p) f -> p t f", p=P)

    with ExitStack() as ctx:
        def sem(name):
            return ctx.enter_context(nc.semaphore(name))

        def allocator(stack):
            return lambda name, shape, dt: stack.enter_context(nc.sbuf_tensor(name, shape, dt))

        sb = allocator(ctx)

        def ps(name, shape, dt=F32):
            return ctx.enter_context(nc.psum_tensor(name, shape, dt))

        ident = sb("ident", [P, P], F32)
        iota_m = sb("iota_m", [P, P], F32)
        iota_0 = sb("iota_0", [P, P], F32)
        iota_1 = sb("iota_1", [P, P], F32)
        ones_b = sb("ones_b", [P, P], BF16)
        ones_f = sb("ones_f", [P, 1], F32)
        left_over = sb("left_over", [P, 1], I32)
        tri = sb("tri", [P, P], BF16)
        stats = sb("stats", [P, KC, GROUPS, 6], F32)
        vec = sb("vec", [P, 3, KC], F32)
        bn_mv = sb("bn_mv", [P, KC, 2], F32)
        bn_t = sb("bn_t", [P, 3, KC], F32)
        bn_scale = sb("bn_scale", [P, KC], F32)
        bn_bias = sb("bn_bias", [P, KC], F32)
        eps_c = sb("eps_c", [P, 1], F32)

        one = ExitStack()
        s1 = allocator(one)
        wT = {(m, part): s1(f"w{m}T_{part}", [P, KC, D], F32R) for m in "lr" for part in ("hi", "lo")}
        vals = s1("vals", [P, WIN, TILES + 1, 6], BF16)
        slot1 = s1("slot1", [P, WIN, TILES + 1], F32)
        dl = s1("dl", [P, WIN, TILES + 1], F32)
        xT_raw = s1("xT_raw", [P, 2, KC, GR], F32)
        xT_hi = s1("xT_hi", [P, 2, KC, GR], F32R)
        xT_lo = s1("xT_lo", [P, 2, KC, GR], F32R)

        zero = ExitStack()
        s0 = allocator(zero)
        w_raw = s0("w_raw", [P, 2, KC, D], F32)
        ends = s0("ends", [BP, 2, BC, EB], I32)
        part_i = s0("part_i", [BP, 4, BC, EB], I32)
        part_b = s0("part_b", [BP, 4, BC, EB], BF16)
        last_f = s0("last_f", [BP, BC], F32)
        d128 = s0("d128", [P, TILES], F32)
        d128_1 = s0("d128_1", [P, TILES], F32)
        before = s0("before", [BP, BC, TILES], BF16)
        first_b = s0("first_b", [P, TILES], F32)
        block_id = s0("block_id", [P, BC, WIN], F32)
        pick = s0("pick", [BP, WIN, BC, TILES], BF16)
        tmp = s0("tmp", [P, 5, TILES], F32)
        in_tile = s0("in_tile", [P, WIN, TILES], F32)
        member = s0("member", [P, WIN, TILES], BF16)
        covered = s0("covered", [P, 2], F32)
        left_f = s0("left_f", [P, 1], F32)
        part_no = s0("part_no", [P, 1], F32)
        row_i = s0("row_i", [P, 3, WIN, TILES], I32)
        e_src = s0("e_src", [P, 1], U32)
        e_dst = s0("e_dst", [P, 1], U32)
        e_row = s0("e_row", [P, P], U32)
        e_dst_f = s0("e_dst_f", [P, 1], F32)
        e_row_f = s0("e_row_f", [P, P], F32)
        same = s0("same", [P, P], F32)
        earlier = s0("earlier", [P, P], F32)
        repeated = s0("repeated", [P, 1], F32)
        e_write = s0("e_write", [P, 1], U32)
        e_x = s0("e_x", [P, CW], F32)
        e_sum = s0("e_sum", [P, CW], F32)
        e_count = s0("e_count", [P, 1], F32)
        zero.close()

        s1 = allocator(one)
        xs = s1("xs", [P, 2, GT, D], F32)
        hot_slot = s1("hot_slot", [P, 2, WIN, P], BF16)
        hot_dst = s1("hot_dst", [P, 2, WIN, P], BF16)
        ct = s1("ct", [P, 4, 8], F32)
        idx_u = s1("idx_u", [P, 4, 1], U32)
        spread = s1("spread", [P, 4, P], F32R)
        rows = s1("rows", [P, 2, D], F32)
        rows_hi = s1("rows_hi", [P, 2, D], F32R)
        rows_lo = s1("rows_lo", [P, 2, D], F32R)
        x_self = s1("x_self", [P, 2, D], F32)
        aggr = s1("aggr", [P, 2, D], F32)
        aT_hi = s1("aT_hi", [P, 2, KC, GR], F32R)
        aT_lo = s1("aT_lo", [P, 2, KC, GR], F32R)
        h_out = s1("h_out", [P, 2, KC, GR], F32)
        one.close()

        two = ExitStack()
        s2 = allocator(two)
        h2 = s2("h2", [P, H2, KC, GR], F32)
        x2 = s2("x2", [P, H2, GT, D], F32)
        r2 = s2("r2", [P, 2, KC, GR], F32)
        o2 = s2("o2", [P, 2, GT, D], F32)
        st2 = s2("st2", [P, 2, GT, 6], F32)
        mv2 = s2("mv2", [P, 2, GT, 2], F32)
        sd2 = s2("sd2", [P, 2, GT, 1], F32)
        rs2 = s2("rs2", [P, 2, GT, 1], F32)
        nm2 = s2("nm2", [P, 2, GT, 1], F32)
        two.close()

        ph = [ps(f"ph{i}", [P, GR]) for i in range(4)]
        paT = [ps(f"paT{i}", [P, KC * P]) for i in range(2)]
        pagg = ps("pagg", [P, D])
        pslot = ps("pslot", [P, 512])
        pwin = [*paT, pagg, pslot]

        s_w = [sem(f"w{m}_loaded") for m in "lr"]
        s_ends = sem("ends_loaded")
        s_vec = sem("vec_loaded")
        s_const = sem("constants_ready")
        s_p0 = sem("prep_vector")
        s_pool0 = sem("pool_step")
        s_wa = sem("windows_copied")
        s_wh = sem("w_hi")
        s_wl = sem("w_lo")
        s_first = sem("first_blocks")
        s_win = sem("windows_picked")
        s_wu = sem("windows_read")
        s_rank = sem("ranks_summed")
        s_pv = sem("prep_vector_step")
        s_gv = sem("general_vector_step")
        s_tab = sem("tables_ready")
        s_cov = sem("covered_counted")
        s_covs = sem("covered_summed")
        s_flag = sem("left_over_ready")
        s_zero = sem("zeros_ready")
        s_zf = sem("sums_cleared")
        s_blk = sem("block_free")
        s_sl = sem("edges_loaded")
        s_eq = sem("same_row_steps")
        s_er = sem("repeats_found")
        s_sg = sem("sources_gathered")
        s_ss = sem("sums_gathered")
        s_sp = sem("block_summed")
        s_sa = sem("sums_added")
        s_sc = sem("sums_scattered")
        s_ml = sem("sums_loaded")
        s_mc = sem("mean_steps")
        s_mm = sem("means_ready")
        s_ms = sem("means_stored")
        s_mnext = sem("means_written")
        s_mdone = sem("general_path_done")
        s_x = [sem(f"x_loaded{b}") for b in range(2)]
        s_xp = sem("x_part_loaded")
        s_xt = [sem(f"xT_loaded{b}") for b in range(2)]
        s_hot = sem("one_hots_built")
        s_comp = sem("slots_filled")
        s_is = sem("slot_steps")
        s_idx = sem("indices_ready")
        s_gat = [sem(f"rows_gathered{b}") for b in range(2)]
        s_go = sem("gather_allowed")
        s_gh = sem("rows_hi_ready")
        s_gl = sem("rows_lo_ready")
        s_agg = sem("rows_summed")
        s_xself = sem("x_self_ready")
        s_aggr = sem("aggr_ready")
        s_xh = sem("xT_hi_ready")
        s_xl = sem("xT_lo_ready")
        s_atr = sem("aggr_transposed")
        s_ah = sem("aT_hi_ready")
        s_al = sem("aT_lo_ready")
        s_main = sem("h_summed")
        s_hc = sem("h_copied")
        s_bn = sem("h_counted")
        s_st = [sem(f"h_stored{b}") for b in range(2)]
        s_stfree = sem("h_out_free")
        s_mz = sem("moments_cleared")
        s_bnv = sem("bn_vector")
        s_bns = sem("bn_root")
        s_bnr = sem("bn_ready")
        s_h2 = [sem(f"h2_loaded{b}") for b in range(H2)]
        s_x2 = [sem(f"x2_loaded{b}") for b in range(H2)]
        s_x2p = sem("x2_part_loaded")
        s_relu = sem("relu_ready")
        s_t2 = sem("relu_transposed")
        s_y = sem("y_ready")
        s_m1 = sem("tile_counted")
        s_all = sem("group_counted")
        s_m2 = sem("moments_ready")
        s_sd = sem("deviation_ready")
        s_rs = sem("inverse_ready")
        s_oa = sem("normalised_by_act")
        s_od = sem("normalised_by_dve")
        s_os = [sem(f"out_stored{b}") for b in range(2)]

        block = ctx.enter_context(nc.Block())

        @block.sync
        def _(sp):
            def load_xT(g, b):
                if isinstance(g, int) and (g + 1) * GR > N:
                    sp.dma_start(xT_raw[:, b, :, 0:N - g * GR], xT_part).then_inc(s_xt[b], 16)
                else:
                    sp.dma_start(xT_raw[:, b], xT_whole[g]).then_inc(s_xt[b], 16)

            sp.dma_start(ends[:, 0], src.rearrange("(c b p) -> b c p", b=BP, p=EB)).then_inc(s_ends, 16)
            sp.dma_start(ends[:, 1], dst.rearrange("(c b p) -> b c p", b=BP, p=EB)).then_inc(s_ends, 16)
            for m, w in ((1, wT_r), (0, wT_l)):
                sp.dma_start(w_raw[:, m], w.rearrange("(c p) f -> p c f", p=P)).then_inc(s_w[m], 16)
            with nc.allow_non_contiguous_dma(reason="three short vectors"):
                for m, v in enumerate((b_l, gamma, beta)):
                    sp.dma_start(vec[:, m], v.rearrange("(c p) -> p c", p=P)).then_inc(s_vec, 16)
            load_xT(0, 0)
            load_xT(1, 1)
            sp.wait_ge(s_flag, 1)
            with sp.If(sp.value_load(left_over[0:1, 0:1], min_val=0, max_val=E) > 0):
                sp.wait_ge(s_zero, 1)
                with sp.Fori(0, TILES - 1) as d:
                    sp.dma_start(sum_dram[bass.ds(d * P, P), :], e_sum[:]).then_inc(s_zf, 16)
                sp.dma_start(sum_dram[N - LAST_ROWS:N, :], e_sum[0:LAST_ROWS, :]).then_inc(s_zf, 16)
                sp.wait_ge(s_zf, 16 * TILES)
                sp.sem_inc(s_blk, 1)
                with sp.Fori(0, NB) as n:
                    sp.wait_ge(s_blk, n + 1)
                    with nc.allow_non_contiguous_dma(reason="an edge to a partition"):
                        for t, e in ((e_src, src), (e_dst, dst)):
                            sp.dma_start(t[0:EB, :], e.bitcast(U32)[bass.ds(n * EB, EB)]
                                         .rearrange("(p o) -> p o", o=1)).then_inc(s_sl, 16)
                    sp.dma_start(e_row[0:EB, 0:EB], dst.bitcast(U32)[bass.ds(n * EB, EB)]
                                 .rearrange("(o p) -> o p", o=1).to_broadcast([EB, EB])).then_inc(s_sl, 16)
                sp.wait_ge(s_blk, NB + 1)

                def mean_tile(d, n):
                    rows = bass.ds(d * P, n)
                    sp.dma_start(e_sum[0:n, :], sum_dram[rows, :]).then_inc(s_ml, 16)
                    sp.wait_ge(s_mm, d + 1)
                    sp.dma_start(mean_dram[rows, :], e_x[0:n, 0:D]).then_inc(s_ms, 16)
                    sp.wait_ge(s_ms, 16 * d + 16)
                    sp.sem_inc(s_mnext, 1)

                with sp.Fori(0, TILES - 1) as d:
                    mean_tile(d, P)
                mean_tile(TILES - 1, LAST_ROWS)
                sp.sem_inc(s_mdone, 1)
            sp.wait_ge(s_tab, 1)

            def load_x(g, b):
                if isinstance(g, int) and (g + 1) * GR > N:
                    full = (N - g * GR) // P
                    lot = sp.dma_start(xs[:, b, 0:full],
                                       x[g * GR:g * GR + full * P, :].rearrange("(t p) f -> p t f", p=P))
                    lot.then_inc(s_x[b], 16)
                    sp.dma_start(xs[0:LAST_ROWS, b, full], x[N - LAST_ROWS:N, :]).then_inc(s_xp, 16)
                else:
                    sp.dma_start(xs[:, b], x_group(g)).then_inc(s_x[b], 16)

            def group(g, b, after):
                if after:
                    sp.wait_ge(s_xl, GT * g + GT)
                    load_xT(g + 2, b)
                    sp.wait_ge(s_xself, GT * g + GT)
                    load_x(g + 2, b)
                sp.wait_ge(s_hc, GT * g + 4 + GT)
                sp.dma_start(h_dram[g], h_out[:, b]).then_inc(s_st[b], 16)
                sp.wait_ge(s_st[b], 8 * (g - b) + 16)
                sp.sem_inc(s_stfree, 1)

            load_x(0, 0)
            load_x(1, 1)
            if PAIRS > 1:
                with sp.Fori(0, PAIRS - 1) as q:
                    for b in range(2):
                        group(2 * q + b, b, True)
            for g in range(2 * PAIRS - 2, GROUPS):
                group(g, g % 2, g + 2 < GROUPS)

            def load2(g, b):
                sp.dma_start(h2[:, b], h_dram[g]).then_inc(s_h2[b], 16)
                if isinstance(g, int) and (g + 1) * GR > N:
                    full = (N - g * GR) // P
                    sp.dma_start(x2[:, b, 0:full],
                                 x[g * GR:g * GR + full * P, :].rearrange("(t p) f -> p t f", p=P)).then_inc(s_x2[b], 16)
                    sp.dma_start(x2[0:LAST_ROWS, b, full], x[N - LAST_ROWS:N, :]).then_inc(s_x2p, 16)
                else:
                    sp.dma_start(x2[:, b], x_group(g)).then_inc(s_x2[b], 16)

            def store2(g, b):
                if isinstance(g, int) and (g + 1) * GR > N:
                    full = (N - g * GR) // P
                    sp.wait_ge(s_oa, 2 * g + 2)
                    sp.wait_ge(s_od, TILES - 2 * (g + 1))
                    sp.dma_start(out[g * GR:g * GR + full * P, :].rearrange("(t p) f -> p t f", p=P),
                                 o2[:, b, 0:full]).then_inc(s_os[b], 16)
                    sp.dma_start(out[N - LAST_ROWS:N, :], o2[0:LAST_ROWS, b, full]).then_inc(s_os[b], 16)
                else:
                    sp.wait_ge(s_oa, 2 * g + 2)
                    sp.wait_ge(s_od, 2 * g + 2)
                    sp.dma_start(out[bass.ds(g * GR, GR), :].rearrange("(t p) f -> p t f", p=P),
                                 o2[:, b]).then_inc(s_os[b], 16)

            sp.wait_ge(s_bnr, 1)
            for g in range(H2):
                load2(g, g)
            rounds2 = (GROUPS - 1 - H2) // H2
            if rounds2 > 0:
                with sp.Fori(0, rounds2) as q:
                    for k in range(H2):
                        store2(H2 * q + k, k % 2)
                        load2(H2 * q + (k + H2), k)
            for g in range(H2 * max(rounds2, 0), GROUPS):
                store2(g, g % 2)
                if g + H2 < GROUPS:
                    load2(g + H2, g % H2)
            for b in range(2):
                stores = len(range(b, GROUPS, 2)) + (b == (GROUPS - 1) % 2)
                sp.wait_ge(s_os[b], 16 * stores)

        @block.tensor
        def _(pe):
            def product(base, c, m, hi, lo, first):
                b, fc = c // GT % 2, c % GT
                u = base + c
                cols = GR
                if isinstance(base, int):
                    cols = min(GR, N - (u // GT) * GR)
                for kc in range(KC):
                    for part, side in (("hi", hi), ("hi", lo), ("lo", hi)):
                        done = not first and kc == KC - 1 and part == "lo"
                        last = pe.matmul(ph[fc][:, 0:cols], wT[m, part][:, kc, fc * P:(fc + 1) * P],
                                         side[:, b, kc, 0:cols],
                                         start=first and kc == 0 and part == "hi" and side is hi, stop=done)
                return last

            pe.wait_ge(s_const, 2)
            pe.wait_ge(s_p0, 1)
            for c in range(BC):
                last = pe.matmul(pslot[:, 0:TILES], ones_b[0:BP, :], before[:, c, :], start=c == 0, stop=c == BC - 1)
            last.then_inc(s_first, 1)
            for j in range(WIN):
                pe.wait_ge(s_p0, 2 + j)
                if j > 0:
                    pe.wait_ge(s_wu, j)
                for a in range(4):
                    for c in range(BC):
                        last = pe.matmul(pwin[a][0:EB, 0:TILES], part_b[:, a, c, :], pick[:, j, c, :],
                                         start=c == 0, stop=c == BC - 1)
                last.then_inc(s_win, 1)
                if j == 0:
                    pe.wait_ge(s_wl, KC)
                    pe.wait_ge(s_xl, GT)
                product(0, j, "r", xT_hi, xT_lo, True)
            pe.wait_ge(s_p0, 2 + WIN)
            for j in range(WIN):
                last = pe.matmul(pwin[j][0:EB, 0:TILES], tri[0:EB, 0:EB], member[0:EB, j, :], start=True, stop=j == 0)
                for k in range(j):
                    last = pe.matmul(pwin[j][0:EB, 0:TILES], ones_b[0:EB, 0:EB], member[0:EB, k, :], start=False,
                                     stop=k == j - 1)
            last.then_inc(s_rank, 1)
            for j in range(WIN, KC):
                product(0, j, "r", xT_hi, xT_lo, True)
            pe.wait_ge(s_cov, 1)
            pe.matmul(pslot[0:1, 0:1], covered[0:EB, 0:1], ones_f[0:EB, :], start=True, stop=True).then_inc(s_covs, 1)
            pe.wait_ge(s_flag, 1)
            with pe.If(pe.value_load(left_over[0:1, 0:1], min_val=0, max_val=E) > 0):
                with pe.Fori(0, NB) as n:
                    pe.wait_ge(s_eq, 3 * n + 2)
                    pe.wait_ge(s_sg, 16 * n + 16)
                    pe.matmul(pagg[0:EB, :], same[0:EB, 0:EB], e_x[0:EB, 0:D], start=True, stop=True)
                    pe.matmul(pslot[0:EB, 0:CW - D], same[0:EB, 0:EB], e_x[0:EB, D:CW], start=True,
                              stop=True).then_inc(s_sp, 1)
            pe.wait_ge(s_tab, 1)

            def fill_slots(base, c):
                i = base + c
                b = c % 2
                pe.wait_ge(s_hot, i + 1)
                if not (isinstance(i, int) and i == 0):
                    pe.wait_ge(s_is, 4 * i - 3)
                for j in range(WIN):
                    pe.matmul(pslot[:, 0:3], hot_slot[0:EB, b, j, :], vals[0:EB, j, i, 0:3],
                              start=j == 0, stop=j == WIN - 1)
                for j in range(WIN):
                    last = pe.matmul(pslot[:, 3:5], hot_dst[0:EB, b, j, :], vals[0:EB, j, i, 3:5],
                                     start=j == 0, stop=j == WIN - 1)
                last.then_inc(s_comp, 1)

            def sum_rows(base, c):
                i = base + c
                b = c % 2
                pe.wait_ge(s_gl, i + 1)
                pe.wait_ge(s_idx, i + 1)
                if not (isinstance(i, int) and i == 0):
                    pe.wait_ge(s_aggr, i)
                pe.matmul(pagg[:], spread[:, c % 4, :], rows_hi[:, b, :], start=True, stop=False)
                pe.matmul(pagg[:], spread[:, c % 4, :], rows_lo[:, b, :], start=False, stop=True).then_inc(s_agg, 1)

            def transpose_aggr(base, c):
                i = base + c
                n = rows_of(i)
                pe.wait_ge(s_aggr, i + 1)
                if not (isinstance(i, int) and i < 2):
                    pe.wait_ge(s_al, i - 1)
                for kc in range(KC):
                    last = pe.transpose(paT[c % 2][:, kc * P:kc * P + n], aggr[0:n, c % 2, kc * P:(kc + 1) * P], ident[0:n, 0:n])
                last.then_inc(s_atr, 1)

            def slot(base, c, main):
                if exists(base + c + 7):
                    fill_slots(base, c + 7)
                if exists(base + c + 5):
                    sum_rows(base, c + 5)
                u = base + c
                ready = GT * (c // GT) + GT + base
                if main and not (isinstance(u, int) and u < GT):
                    pe.wait_ge(s_hc, u + 1)
                    if c % GT == 0:
                        pe.wait_ge(s_xl, ready)
                    product(base, c, "r", xT_hi, xT_lo, True)
                if exists(base + c + 4):
                    transpose_aggr(base, c + 4)
                if main:
                    if c == 0 and isinstance(base, int):
                        pe.wait_ge(s_wl, 2 * KC)
                    if c % GT == 0:
                        pe.wait_ge(s_al, min(ready, TILES) if isinstance(ready, int) else ready)
                    product(base, c, "l", aT_hi, aT_lo, False).then_inc(s_main, 1)

            for c in range(-8, LOOP):
                slot(0, c, c >= 0)
            with pe.Fori(1, PAIRS) as q:
                for c in range(LOOP):
                    slot(LOOP * q, c, True)
            for c in range(GROUPS * GT - REST):
                slot(REST, c, True)

            def back(g, b, cols):
                for t in range(-(-cols // P)):
                    n = min(P, cols - t * P)
                    if t == 0:
                        pe.wait_ge(s_relu, GT * g + GT)
                    if not isinstance(g, int) or g > 0:
                        pe.wait_ge(s_y, GT * g + t - 3)
                    for fc in range(KC):
                        last = pe.transpose(ph[t][0:n, fc * P:(fc + 1) * P], r2[:, b, fc, t * P:t * P + n], ident[:])
                    last.then_inc(s_t2, 1)

            for g in range(2):
                back(g, g, GR)
            with pe.Fori(1, PAIRS) as q:
                for b in range(2):
                    back(2 * q + b, b, GR)
            for g in range(2 * PAIRS, GROUPS):
                back(g, g % 2, min(GR, N - g * GR))

        @block.scalar
        def _(act):
            def w_hi(m):
                act.wait_ge(s_w["lr".index(m)], 16)
                for kc in range(KC):
                    act.activation(wT[m, "hi"][:, kc, :], w_raw[:, "lr".index(m), kc, :], ACT.Copy).then_inc(s_wh, 1)

            def x_hi(base, c):
                i = base + c
                b, kc = c // GT % 2, c % GT
                cols = min(GR, N - (i // GT) * GR) if isinstance(i, int) else GR
                act.wait_ge(s_xt[b], 2 * base + 16 * (c // LOOP) + 16)
                if not (isinstance(i, int) and i < LOOP):
                    act.wait_ge(s_main, GT * (c // GT) + base - GT)
                act.activation(xT_hi[:, b, kc, 0:cols], xT_raw[:, b, kc, 0:cols], ACT.Copy).then_inc(s_xh, 1)

            w_hi("r")
            for c in range(GT):
                x_hi(0, c)
            w_hi("l")
            for j in range(WIN):
                act.wait_ge(s_win, j + 1)
                a = slice(0, EB)
                sh, slo, dh, dlo = (pwin[k][a, 0:TILES] for k in range(4))
                act.activation(tmp[a, 1], dlo, ACT.Copy)
                act.activation(tmp[a, 0], slo, ACT.Copy, bias=1.0)
                act.activation(vals[a, j, 0:TILES, 1], slo, ACT.Copy)
                act.activation(vals[a, j, 0:TILES, 0], sh, ACT.Copy, bias=-256.0).then_inc(s_wa, 1)
            act.sem_inc(s_hc, 4)
            act.sem_inc(s_stfree, 2)
            act.wait_ge(s_tab, 1)
            act.wait_ge(s_vec, 48)

            def self_share(base, c):
                i = base + c
                b, t, n = c // GT % 2, c % GT, rows_of(i)
                act.wait_ge(s_x[b], 2 * base + 16 * (c // LOOP) + 16)
                if n < P:
                    act.wait_ge(s_xp, 16)
                act.wait_ge(s_is, 4 * i + 4)
                if not (isinstance(i, int) and i < 2):
                    act.wait_ge(s_aggr, i - 1)
                act.activation(x_self[0:n, c % 2, :], xs[0:n, b, t, :], ACT.Copy,
                               scale=ct[0:n, c % 4, 7:8]).then_inc(s_xself, 1)

            def hi_of(base, c, bank, ready, side, done):
                i = base + c
                b, t, n = c // GT % 2, c % GT, rows_of(i)
                act.wait_ge(ready, i + 1)
                if not (isinstance(i, int) and i < LOOP):
                    act.wait_ge(s_main, GT * (c // GT) + base - GT)
                part = bank[c % 2][:, 0:KC * P].rearrange("p (c r) -> p c r", c=KC)[:, :, 0:n]
                act.activation(side[:, b, :, t * P:t * P + n], part, ACT.Copy).then_inc(done, 1)

            def rows_high(base, c):
                i = base + c
                if isinstance(i, int):
                    act.wait_ge(s_gat[c % 2], 16 * (i // 2 + 1))
                else:
                    act.wait_ge(s_gat[c % 2], 8 * base + 16 * (c // 2 + 1))
                if not (isinstance(i, int) and i < 2):
                    act.wait_ge(s_agg, i - 1)
                act.activation(rows_hi[:, c % 2, :], rows[:, c % 2, :], ACT.Copy).then_inc(s_gh, 1)

            def copy_h(base, c):
                u = base + c
                b, fc = c // GT % 2, c % GT
                cols = min(GR, N - (u // GT) * GR) if isinstance(base, int) else GR
                act.wait_ge(s_main, u + 1)
                if fc == 0:
                    g1 = c // GT + (base // GT if isinstance(base, int) else q2[0])
                    act.wait_ge(s_stfree, g1 + 1)
                    act.wait_ge(s_bn, GT * g1 + GT)
                act.activation(h_out[:, b, fc, 0:cols], ph[fc][:, 0:cols], ACT.Identity,
                               bias=vec[:, 0, fc:fc + 1]).then_inc(s_hc, 1)

            q2 = [0]

            def slot(base, c, main):
                if exists(base + c + 5):
                    self_share(base, c + 5)
                for k in x_chunks(base, c):
                    x_hi(base, k)
                if exists(base + c + 4):
                    hi_of(base, c + 4, paT, s_atr, aT_hi, s_ah)
                if exists(base + c + 6):
                    rows_high(base, c + 6)
                if main:
                    copy_h(base, c)

            for c in range(-8, LOOP):
                slot(0, c, c >= 0)
            with act.Fori(1, PAIRS) as q:
                q2[0] = 2 * q
                for c in range(LOOP):
                    slot(LOOP * q, c, True)
            for c in range(GROUPS * GT - REST):
                slot(REST, c, True)

            act.wait_ge(s_bnv, 1)
            act.activation(bn_t[:, 0, :], bn_mv[:, :, 1], ACT.Sqrt, bias=eps_c[:]).then_inc(s_bns, 1)
            act.wait_ge(s_bnr, 1)

            def relu(g, k, loaded, cols):
                b = k % 2
                act.wait_ge(s_h2[k % H2], loaded)
                if not isinstance(g, int) or g >= 2:
                    act.wait_ge(s_t2, GT * g - GT)
                for fc in range(KC):
                    act.activation(r2[:, b, fc, 0:cols], h2[:, k % H2, fc, 0:cols], ACT.Relu,
                                   bias=bn_bias[:, fc:fc + 1], scale=bn_scale[:, fc:fc + 1]).then_inc(s_relu, 1)

            def root(g, k):
                b = k % 2
                act.wait_ge(s_m2, GT * g + GT)
                act.activation(sd2[:, b, :, 0], mv2[:, b, :, 1], ACT.Sqrt, bias=eps_c[:]).then_inc(s_sd, 1)

            def normalise(g, k):
                b = k % 2
                act.wait_ge(s_rs, 2 * g + 2)
                if not isinstance(g, int) or g >= 2:
                    act.wait_ge(s_os[b], 8 * (g - b))
                for t in range(2):
                    act.activation(o2[:, b, t, :], x2[:, k % H2, t, :], ACT.Identity, bias=nm2[:, b, t, :],
                                   scale=rs2[:, b, t, :]).then_inc(s_oa, 1)

            def step2(g, k, loaded):
                if not isinstance(g, int) or g + 1 < GROUPS:
                    relu(g + 1, k + 1, loaded, min(GR, N - (g + 1) * GR) if isinstance(g, int) else GR)
                if not isinstance(g, int) or g > 0:
                    normalise(g - 1, k - 1)
                if not isinstance(g, int) or g < GROUPS:
                    root(g, k)

            relu(0, 0, 16, GR)
            for g in range(H2):
                step2(g, g, 16 * ((g + 1) // H2) + 16)
            if ROUNDS2 > 1:
                with act.Fori(1, ROUNDS2) as q:
                    for k in range(H2):
                        step2(H2 * q + k, k, 16 * q + 16 * ((k + 1) // H2) + 16)
            for g in range(H2 * max(ROUNDS2, 1), GROUPS + 1):
                step2(g, g, 16 * ((g + 1) // H2) + 16)

        @block.vector
        def _(dve):
            steps = {s_pv: 0, s_gv: 0}

            def link(ins, s=s_pv):
                steps[s] += 1
                ins.then_inc(s, 1)
                dve.wait_ge(s, steps[s])

            dve.memset(eps_c[:], EPS)
            dve.memset(vals[:, :, :, 3:4], 1.0)
            dve.memset(ones_f[:], 1.0)
            dve.wait_ge(s_ends, 32)
            dve.wait_ge(s_const, 2)
            dve.tensor_copy(last_f[:], ends[:, 1, :, EB - 1])
            link(dve.tensor_scalar(part_i[:, 0], ends[:, 1], 1, None, ALU.add))
            link(dve.tensor_scalar(part_i[:, 2], part_i[:, 0], 8, None, ALU.logical_shift_right))
            link(dve.tensor_scalar(part_i[:, 3], part_i[:, 0], 255, None, ALU.bitwise_and))
            link(dve.tensor_scalar(part_i[:, 0], ends[:, 0], 8, None, ALU.logical_shift_right))
            link(dve.tensor_scalar(part_i[:, 1], ends[:, 0], 255, None, ALU.bitwise_and))
            link(dve.tensor_copy(part_b[:], part_i[:]))
            for c in range(BC):
                last = dve.tensor_scalar(before[:, c, :], d128[0:BP, :], last_f[:, c:c + 1], None, ALU.is_gt)
            last.then_inc(s_p0, 1)
            dve.wait_ge(s_first, 1)
            link(dve.tensor_copy(first_b[:], pslot[:, 0:TILES]))
            for j in range(WIN):
                for c in range(BC):
                    last = dve.tensor_scalar(pick[:, j, c, :], first_b[0:BP, :], block_id[0:BP, c, j:j + 1], None,
                                             ALU.is_equal)
                last.then_inc(s_p0, 1)
            a = slice(0, EB)
            for j in range(WIN):
                dve.wait_ge(s_wa, j + 1)
                dve.scalar_tensor_tensor(tmp[a, 2], pwin[0][a, 0:TILES], 256.0, tmp[a, 0], ALU.mult, ALU.add)
                dve.scalar_tensor_tensor(tmp[a, 3], pwin[2][a, 0:TILES], 256.0, tmp[a, 1],
                                         ALU.mult, ALU.add).then_inc(s_wu, 1)
                dve.wait_ge(s_wu, j + 1)
                dve.tensor_tensor(vals[a, j, 0:TILES, 4], tmp[a, 2], tmp[a, 3], ALU.is_equal)
                link(dve.tensor_tensor(dl[a, j, 0:TILES], tmp[a, 3], d128_1[a, :], ALU.subtract))
                dve.tensor_scalar(vals[a, j, 0:TILES, 2], dl[a, j, 0:TILES], float(P), None, ALU.subtract)
                link(dve.tensor_scalar(tmp[a, 4], dl[a, j, 0:TILES], 0.0, None, ALU.is_ge))
                link(dve.scalar_tensor_tensor(in_tile[a, j, :], dl[a, j, 0:TILES], float(P), tmp[a, 4],
                                              ALU.is_lt, ALU.mult))
                last = dve.scalar_tensor_tensor(member[a, j, :], vals[a, j, 0:TILES, 4], 0.5, in_tile[a, j, :],
                                                ALU.is_lt, ALU.mult)
            last.then_inc(s_p0, 1)
            dve.wait_ge(s_rank, 1)
            for j in range(WIN):
                last = dve.scalar_tensor_tensor(slot1[a, j, 0:TILES], pwin[j][a, 0:TILES], 1.0, member[a, j, :],
                                                ALU.add, ALU.mult)
            link(last)
            link(dve.tensor_reduce(covered[a, 0:1], in_tile[a], AX.XY, ALU.add))
            link(dve.tensor_scalar(in_tile[a], slot1[a, :, 0:TILES], float(P), None, ALU.is_gt))
            link(dve.tensor_reduce(covered[a, 1:2], in_tile[a], AX.XY, ALU.add))
            dve.tensor_tensor(covered[a, 0:1], covered[a, 0:1], covered[a, 1:2], ALU.subtract).then_inc(s_cov, 1)
            dve.wait_ge(s_covs, 1)
            link(dve.tensor_scalar(left_f[0:1, :], pslot[0:1, 0:1], -1.0, float(E), ALU.mult, ALU.add))
            dve.tensor_copy(left_over[0:1, :], left_f[0:1, :]).then_inc(s_flag, 1)
            dve.wait_ge(s_flag, 1)
            with dve.If(dve.value_load(left_over[0:1, 0:1], min_val=0, max_val=E) > 0):
                link(dve.memset(e_x[:], 1.0), s_gv)
                dve.memset(e_sum[:], 0.0).then_inc(s_zero, 1)
                with dve.Fori(0, NB) as n:
                    dve.wait_ge(s_sl, 48 * n + 48)
                    dve.tensor_copy(e_row_f[a, 0:EB], e_row[a, 0:EB])
                    dve.tensor_copy(e_dst_f[a], e_dst[a]).then_inc(s_eq, 1)
                    dve.wait_ge(s_eq, 3 * n + 1)
                    dve.tensor_scalar(same[a, 0:EB], e_row_f[a, 0:EB], e_dst_f[a], None, ALU.is_equal).then_inc(s_eq, 1)
                    dve.wait_ge(s_eq, 3 * n + 2)
                    dve.scalar_tensor_tensor(earlier[a, 0:EB], iota_0[a, 0:EB], part_no[a], same[a, 0:EB],
                                             ALU.is_lt, ALU.mult).then_inc(s_eq, 1)
                    dve.wait_ge(s_eq, 3 * n + 3)
                    dve.tensor_reduce(repeated[a], earlier[a, 0:EB], AX.X, ALU.max).then_inc(s_er, 1)
                    dve.wait_ge(s_er, n + 1)
                    dve.scalar_tensor_tensor(e_write[a], repeated[a], float(EMPTY), e_dst_f[a], ALU.mult, ALU.add)
                    dve.wait_ge(s_sp, n + 1)
                    dve.wait_ge(s_ss, 16 * n + 16)
                    dve.tensor_tensor(e_sum[a, 0:D], pagg[a, :], e_sum[a, 0:D], ALU.add)
                    dve.tensor_tensor(e_sum[a, D:CW], pslot[a, 0:CW - D], e_sum[a, D:CW], ALU.add).then_inc(s_sa, 1)

                def mean_tile(d, n):
                    dve.wait_ge(s_ml, 16 * d + 16)
                    dve.tensor_scalar(e_count[0:n], e_sum[0:n, D:D + 1], 1.0, None, ALU.max).then_inc(s_mc, 1)
                    dve.wait_ge(s_mc, 2 * d + 1)
                    dve.reciprocal(e_count[0:n], e_count[0:n]).then_inc(s_mc, 1)
                    dve.wait_ge(s_mc, 2 * d + 2)
                    dve.tensor_scalar(e_x[0:n, 0:D], e_sum[0:n, 0:D], e_count[0:n], None, ALU.mult).then_inc(s_mm, 1)

                with dve.Fori(0, TILES - 1) as d:
                    mean_tile(d, P)
                mean_tile(TILES - 1, LAST_ROWS)
                dve.wait_ge(s_mdone, 1)
                dve.tensor_scalar(row_i[a, 1], row_i[a, 0], 8, None, ALU.logical_shift_right)
                link(dve.tensor_scalar(row_i[a, 2], row_i[a, 0], 255, None, ALU.bitwise_and), s_gv)
                for j in range(WIN):
                    dve.tensor_scalar(vals[a, j, 0:TILES, 0], row_i[a, 1, j], 256.0, None, ALU.subtract)
                    dve.tensor_copy(vals[a, j, 0:TILES, 1], row_i[a, 2, j])
                    link(dve.tensor_copy(in_tile[a, j], row_i[a, 0, j]), s_gv)
                    link(dve.tensor_tensor(dl[a, j, 0:TILES], in_tile[a, j], d128[a, :], ALU.subtract), s_gv)
                    dve.tensor_scalar(vals[a, j, 0:TILES, 2], dl[a, j, 0:TILES], float(P), None, ALU.subtract)
                    dve.tensor_scalar(slot1[a, j, 0:TILES], dl[a, j, 0:TILES], 1.0, None, ALU.add)
                link(dve.memset(vals[:, :, :, 4:5], 0.0), s_gv)
            dve.wait_ge(s_wl, 2 * KC)
            dve.memset(slot1[:, :, TILES:TILES + 1], 0.0)
            dve.memset(dl[:, :, TILES:TILES + 1], -1.0).then_inc(s_tab, 1)
            dve.sem_inc(s_bn, 8)
            dve.wait_ge(s_tab, 1)

            def one_hots(base, c):
                i = base + c
                b = c % 2
                if not (isinstance(i, int) and i < 2):
                    dve.wait_ge(s_comp, i - 1)
                for j in range(WIN):
                    dve.tensor_scalar(hot_slot[a, b, j, :], iota_1[a, :], slot1[a, j, bass.ds(i, 1)], None, ALU.is_equal)
                for j in range(WIN):
                    last = dve.tensor_scalar(hot_dst[a, b, j, :], iota_0[a, :], dl[a, j, bass.ds(i, 1)], None, ALU.is_equal)
                last.then_inc(s_hot, 1)

            def indices(base, c):
                i = base + c
                k = c % 4
                dve.wait_ge(s_comp, i + 1)
                dve.tensor_copy(ct[:, k, 0:5], pslot[:, 0:5]).then_inc(s_is, 1)
                dve.wait_ge(s_is, 4 * i + 1)
                dve.scalar_tensor_tensor(ct[:, k, 5:6], ct[:, k, 0:1], 256.0, ct[:, k, 1:2], ALU.mult, ALU.add)
                dve.tensor_scalar(ct[:, k, 6:7], ct[:, k, 3:4], 1.0, None, ALU.max).then_inc(s_is, 1)
                dve.wait_ge(s_is, 4 * i + 2)
                dve.tensor_scalar(idx_u[:, k, :], ct[:, k, 5:6], float(EMPTY), None, ALU.add)
                dve.reciprocal(ct[:, k, 6:7], ct[:, k, 6:7]).then_inc(s_is, 1)
                dve.tensor_scalar(spread[:, k, :], iota_m[:], ct[:, k, 2:3], None, ALU.is_equal).then_inc(s_idx, 1)
                dve.wait_ge(s_is, 4 * i + 3)
                dve.tensor_tensor(ct[:, k, 7:8], ct[:, k, 4:5], ct[:, k, 6:7], ALU.mult).then_inc(s_is, 1)

            def mean(base, c):
                i = base + c
                n = rows_of(i)
                dve.wait_ge(s_agg, i + 1)
                dve.wait_ge(s_xself, i + 1)
                if not (isinstance(i, int) and i < 2):
                    dve.wait_ge(s_atr, i - 1)
                dve.scalar_tensor_tensor(aggr[0:n, c % 2, :], pagg[0:n, :], ct[0:n, c % 4, 6:7], x_self[0:n, c % 2, :],
                                         ALU.mult, ALU.add).then_inc(s_aggr, 1)

            def lo_of(base, c, bank, ready, hi, lo, done):
                i = base + c
                b, t, n = c // GT % 2, c % GT, rows_of(i)
                dve.wait_ge(ready, i + 1)
                part = bank[c % 2][:, 0:KC * P].rearrange("p (c r) -> p c r", c=KC)[:, :, 0:n]
                dve.tensor_tensor(lo[:, b, :, t * P:t * P + n], part,
                                  hi[:, b, :, t * P:t * P + n].bitcast(F32), ALU.subtract).then_inc(done, 1)

            def count_h(base, c):
                u = base + c
                fc = c % GT
                cols = min(GR, N - (u // GT) * GR) if isinstance(base, int) else GR
                g = c // GT + (base // GT if isinstance(base, int) else q2[0])
                dve.wait_ge(s_hc, u + 5)
                dve.bn_stats(stats[:, fc, g, :], h_out[:, c // GT % 2, fc, 0:cols]).then_inc(s_bn, 1)

            q2 = [0]

            def slot(base, c, main):
                if exists(base + c + 7):
                    indices(base, c + 7)
                if exists(base + c + 5):
                    mean(base, c + 5)
                if exists(base + c + 8):
                    one_hots(base, c + 8)
                if exists(base + c + 4):
                    lo_of(base, c + 4, paT, s_ah, aT_hi, aT_lo, s_al)
                if main:
                    count_h(base, c)

            for c in range(-8, 0):
                slot(0, c, False)
            with dve.Fori(0, PAIRS) as q:
                q2[0] = 2 * q
                for c in range(LOOP):
                    slot(LOOP * q, c, True)
            for c in range(GROUPS * GT - REST):
                slot(REST, c, True)

            dve.wait_ge(s_bn, GROUPS * GT + 8)
            dve.wait_ge(s_vec, 48)
            for fc in range(KC):
                last = dve.bn_aggr(bn_mv[:, fc, :], stats[:, fc].rearrange("p g s -> p (g s)"))
            last.then_inc(s_bnv, 1)
            dve.wait_ge(s_bns, 1)
            link(dve.reciprocal(bn_t[:, 1, :], bn_t[:, 0, :]))
            link(dve.tensor_tensor(bn_scale[:], bn_t[:, 1, :], vec[:, 1, :], ALU.mult))
            link(dve.tensor_tensor(bn_t[:, 2, :], bn_mv[:, :, 0], bn_scale[:], ALU.mult))
            dve.tensor_tensor(bn_bias[:], vec[:, 2, :], bn_t[:, 2, :], ALU.subtract).then_inc(s_bnr, 1)

            def sum_y(g, k, loaded, cols):
                b, tiles = k % 2, -(-cols // P)
                for t in range(tiles):
                    n = min(P, cols - t * P)
                    dve.wait_ge(s_t2, GT * g + t + 1)
                    if t == 0:
                        dve.wait_ge(s_x2[k % H2], loaded)
                    if n < P:
                        dve.wait_ge(s_x2p, 16)
                    dve.tensor_tensor(x2[0:n, k % H2, t, :], ph[t][0:n, :], x2[0:n, k % H2, t, :],
                                      ALU.add).then_inc(s_y, 1)
                if not isinstance(g, int) or g >= 2:
                    dve.wait_ge(s_oa, 2 * g - 2)
                for t in range(tiles):
                    n = min(P, cols - t * P)
                    dve.wait_ge(s_y, GT * g + t + 1)
                    dve.bn_stats(st2[0:n, b, t, :], x2[0:n, k % H2, t, :]).then_inc(s_m1, 1)
                dve.wait_ge(s_m1, GT * g + tiles)
                dve.sem_inc(s_all, 1)
                for t in range(tiles):
                    n = min(P, cols - t * P)
                    last = dve.bn_aggr(mv2[0:n, b, t, :], st2[0:n, b, t, :])
                    last.then_inc(s_m2, 1 if t < tiles - 1 else GT - tiles + 1)

            def invert(g, k):
                b = k % 2
                dve.wait_ge(s_sd, g + 1)
                dve.reciprocal(rs2[:, b], sd2[:, b]).then_inc(s_rs, 1)
                dve.wait_ge(s_rs, 2 * g + 1)
                dve.scalar_tensor_tensor(nm2[:, b, :, 0], mv2[:, b, :, 0], -1.0, rs2[:, b, :, 0],
                                         ALU.mult, ALU.mult).then_inc(s_rs, 1)

            def normalise(g, k):
                b = k % 2
                dve.wait_ge(s_rs, 2 * g + 2)
                if not isinstance(g, int) or g >= 2:
                    dve.wait_ge(s_os[b], 8 * (g - b))
                for t in range(2, GT):
                    n = min(P, N - g * GR - t * P) if isinstance(g, int) else P
                    if n > 0:
                        dve.tensor_scalar(o2[0:n, b, t, :], x2[0:n, k % H2, t, :], mv2[0:n, b, t, 0:1],
                                          rs2[0:n, b, t, :], ALU.subtract, ALU.mult).then_inc(s_od, 1)

            def step2(g, k, loaded):
                if not isinstance(g, int) or g < GROUPS:
                    sum_y(g, k, loaded, min(GR, N - g * GR) if isinstance(g, int) else GR)
                if not isinstance(g, int) or g > 0:
                    normalise(g - 1, k - 1)
                if not isinstance(g, int) or g < GROUPS:
                    invert(g, k)

            dve.memset(mv2[:], 1.0).then_inc(s_mz, 1)
            dve.wait_ge(s_mz, 1)
            for g in range(H2):
                step2(g, g, 16)
            if ROUNDS2 > 1:
                with dve.Fori(1, ROUNDS2) as q:
                    for k in range(H2):
                        step2(H2 * q + k, k, 16 * q + 16)
            for g in range(H2 * max(ROUNDS2, 1), GROUPS + 1):
                step2(g, g, 16 * (g // H2) + 16)

        @block.gpsimd
        def _(pool):
            def number(t, pattern, base, channel):
                return pool.iota(t, pattern, base=base, channel_multiplier=channel, allow_small_or_imprecise_dtypes=True)

            pool.memset(ident[:], 0.0)
            pool.memset(tri[:], 1.0)
            pool.memset(ones_b[:], 1.0).then_inc(s_pool0, 1)
            pool.wait_ge(s_pool0, 1)
            pool.affine_select(out=ident[:], in_=ident[:], compare_op=ALU.not_equal, fill=1.0, base=0,
                               pattern=[[-1, P]], channel_multiplier=1).then_inc(s_const, 1)
            pool.affine_select(out=tri[:], in_=tri[:], compare_op=ALU.is_gt, fill=0.0, base=0,
                               pattern=[[1, P]], channel_multiplier=-1)
            number(d128[:], [[P, TILES]], 0, 0)
            number(d128_1[:], [[P, TILES]], 1, 0)
            number(block_id[:], [[BP, BC], [-1, WIN]], 0, 1)
            number(row_i[:, 0], [[EB, WIN], [P, TILES]], 0, 1)
            number(part_no[:], [[0, 1]], 0, 1)
            number(iota_m[:], [[1, P]], -P, 0)
            number(iota_0[:], [[1, P]], 0, 0)
            number(iota_1[:], [[1, P]], 1, 0).then_inc(s_const, 1)

            def w_lo(m):
                for kc in range(KC):
                    pool.wait_ge(s_wh, ("rl".index(m)) * KC + kc + 1)
                    pool.tensor_tensor(wT[m, "lo"][:, kc, :], w_raw[:, "lr".index(m), kc, :],
                                       wT[m, "hi"][:, kc, :].bitcast(F32), ALU.subtract).then_inc(s_wl, 1)

            def x_lo(base, c):
                i = base + c
                b, kc = c // GT % 2, c % GT
                cols = min(GR, N - (i // GT) * GR) if isinstance(i, int) else GR
                pool.wait_ge(s_xh, i + 1)
                pool.tensor_tensor(xT_lo[:, b, kc, 0:cols], xT_raw[:, b, kc, 0:cols],
                                   xT_hi[:, b, kc, 0:cols].bitcast(F32), ALU.subtract).then_inc(s_xl, 1)

            w_lo("r")
            for c in range(GT):
                x_lo(0, c)
            w_lo("l")
            pool.wait_ge(s_flag, 1)
            left = pool.value_load(left_over[0:1, 0:1], min_val=0, max_val=E)

            def indexed(out, table, of, index, scatter=False):
                by = bass.IndirectOffsetOnAxis(ap=index, axis=0)
                return pool.indirect_dma_start(out=table if scatter else out, out_offset=by if scatter else None,
                                               in_=out if scatter else table, in_offset=None if scatter else by,
                                               bounds_check=of - 1, oob_is_err=False)

            with pool.If(left > 0):
                pool.wait_ge(s_zf, 16 * TILES)
                with pool.Fori(0, NB) as n:
                    pool.wait_ge(s_sl, 48 * n + 48)
                    pool.sem_inc(s_go, 1)
                    indexed(e_x[0:EB, 0:D], x[:, :], N, e_src[0:EB, :]).then_inc(s_sg, 16)
                    indexed(e_sum[0:EB, :], sum_dram[:, :], N, e_dst[0:EB, :]).then_inc(s_ss, 16)
                    pool.wait_ge(s_sa, n + 1)
                    pool.sem_inc(s_go, 1)
                    indexed(e_sum[0:EB, :], sum_dram[:, :], N, e_write[0:EB, :], scatter=True).then_inc(s_sc, 16)
                    pool.wait_ge(s_sc, 16 * n + 16)
                    pool.sem_inc(s_blk, 1)
            pool.wait_ge(s_tab, 1)
            pool.memset(rows[:], 0.0).then_inc(s_pool0, 1)
            pool.wait_ge(s_pool0, 2)

            last_row = pool.alloc_register("last_row")
            pool.reg_mov(last_row, N - 1)

            def gather(base, c):
                i = base + c
                pool.wait_ge(s_idx, i + 1)
                if not (isinstance(i, int) and i < 2):
                    pool.wait_ge(s_gl, i - 1)
                pool.sem_inc(s_go, 1)
                with pool.If(left > 0):
                    indexed(rows[:, c % 2, :], mean_dram[:, :], N, idx_u[:, c % 4, :]).then_inc(s_gat[c % 2], 16)
                with pool.Else():
                    indexed(rows[:, c % 2, :], x[:, :], N, idx_u[:, c % 4, :]).then_inc(s_gat[c % 2], 16)

            def rows_low(base, c):
                i = base + c
                pool.wait_ge(s_gh, i + 1)
                pool.tensor_tensor(rows_lo[:, c % 2, :], rows[:, c % 2, :], rows_hi[:, c % 2, :].bitcast(F32),
                                   ALU.subtract).then_inc(s_gl, 1)

            def slot(base, c):
                if exists(base + c + 7):
                    gather(base, c + 7)
                if exists(base + c + 6):
                    rows_low(base, c + 6)
                for k in x_chunks(base, c):
                    x_lo(base, k)

            for c in range(-8, 0):
                slot(0, c)
            with pool.Fori(0, PAIRS) as q:
                for c in range(LOOP):
                    slot(LOOP * q, c)
            for c in range(TILES - REST):
                slot(REST, c)


def kernel(**inputs):
    import numpy as np
    import concourse.bacc as bacc
    from concourse.bass_utils import run_bass_kernel_spmd

    x = inputs["x"]
    n, d = x.shape
    whole = n // GR * GR
    arrays = {
        "x": x,
        "xT_whole": x[:whole].reshape(n // GR, GR, d // P, P).transpose(0, 3, 2, 1),
        "xT_part": x[whole:].reshape(n - whole, d // P, P).transpose(2, 1, 0),
        "src": inputs["src"],
        "dst": inputs["dst"],
        "wT_l": inputs["L0_gnn_W_l"].T,
        "b_l": inputs["L0_gnn_b_l"],
        "wT_r": inputs["L0_gnn_W_r"].T,
        "gamma": inputs["L0_gnn_gamma"],
        "beta": inputs["L0_gnn_beta"],
    }
    arrays = {name: np.ascontiguousarray(a) for name, a in arrays.items()}
    nc = bacc.Bacc("TRN2", target_bir_lowering=False, num_devices=1)
    args = [nc.dram_tensor(name, a.shape, mybir.dt.from_np(a.dtype), kind="ExternalInput").ap()
            for name, a in arrays.items()]
    out = nc.dram_tensor("out", x.shape, F32, kind="ExternalOutput").ap()
    bass_sage_batchnorm_residual_layernorm_kernel(nc, *args, out)
    return run_bass_kernel_spmd(nc, [arrays], core_ids=[0]).results[0]["out"]
```

```python
from contextlib import ExitStack

import concourse.bass as bass
from concourse import mybir

ALU = mybir.AluOpType
ACT = mybir.ActivationFunctionType
AX = mybir.AxisListType
F32 = mybir.dt.float32
F32R = mybir.dt.float32r
BF16 = mybir.dt.bfloat16
I32 = mybir.dt.int32
U32 = mybir.dt.uint32

P = 128
GT = 4
GR = GT * P
WIN = 3
LOOP = 2 * GT
H2 = 8
OB = 4
KEPT = 2
EARLY = 2
EPS = 1e-5


def largest_divisor(n, most):
    return max(k for k in range(1, most + 1) if n % k == 0)


def bass_sage_batchnorm_residual_layernorm_kernel(
    nc, x, xT_whole, xT_part, src, dst, wT_l, b_l, wT_r, gamma, beta, out
):
    N, D = x.shape
    E = src.shape[0]
    KC = D // P
    TILES = -(-N // P)
    GROUPS = -(-TILES // GT)
    LAST_ROWS = N - (TILES - 1) * P
    EB = largest_divisor(E, P)
    NB = E // EB
    BP = largest_divisor(NB, P)
    BC = NB // BP
    PAIRS = (GROUPS - 1) // 2
    ROUNDS2 = (GROUPS - 1) // H2
    REST = LOOP * PAIRS
    EMPTY = 1 << 16
    assert D == KC * P and KC == GT and N < EMPTY and TILES <= 512
    assert WIN * EB >= P
    assert GROUPS % KEPT == 0 and H2 % OB == 0 and H2 % 2 == 0 and GROUPS > 2 * H2 and N - (GROUPS - 1) * GR >= 2 * P
    assert REST + 7 >= TILES and REST + LOOP >= GROUPS * GT - GT + 1 and PAIRS >= 1

    def rows_of(i):
        return LAST_ROWS if isinstance(i, int) and i == TILES - 1 else P

    def chunk_exists(i):
        return not isinstance(i, int) or i < GROUPS * GT

    def x_chunks(base, c):
        first = c - c % GT + GT
        chunks = ((0,), (1,), (2, 3), ())[c % GT]
        return [first + k for k in chunks if chunk_exists(base + first) and not (
            isinstance(base, int) and base + first < GT)]

    def exists(i):
        return not isinstance(i, int) or 0 <= i < TILES

    def group_of(k):
        return GROUPS - KEPT + k if isinstance(k, int) and k < KEPT else k - KEPT

    def cols_of(k):
        return N - (GROUPS - 1) * GR if isinstance(k, int) and k == KEPT - 1 else GR

    def loaded(q, k):
        return 16 * q + 16 * (k // H2) + (16 if k % H2 >= KEPT else 0)

    def out_free(q, k):
        return 16 * (H2 // OB * q + k // OB) + (16 if k % OB == KEPT - 1 else 0)

    CW = D + 8
    sum_dram = nc.dram_tensor("sum_scratch", (N, CW), F32).ap()
    mean_dram = nc.dram_tensor("mean_scratch", (N, D), F32).ap()
    h_dram = nc.dram_tensor("h_scratch", (GROUPS, P, KC, GR), F32).ap()

    def x_group(g):
        return x[bass.ds(g * GR, GR), :].rearrange("(t p) f -> p t f", p=P)

    with ExitStack() as ctx:
        def sem(name):
            return ctx.enter_context(nc.semaphore(name))

        def allocator(stack, side="left"):
            return lambda name, shape, dt: stack.enter_context(nc.sbuf_tensor(name, shape, dt, side=side))

        sb = allocator(ctx)

        def ps(name, shape, dt=F32):
            return ctx.enter_context(nc.psum_tensor(name, shape, dt))

        ident = sb("ident", [P, P], F32)
        iota_m = sb("iota_m", [P, P], F32)
        iota_0 = sb("iota_0", [P, P], F32)
        iota_1 = sb("iota_1", [P, P], F32)
        ones_b = sb("ones_b", [P, P], BF16)
        ones_f = sb("ones_f", [P, 1], F32)
        left_over = sb("left_over", [P, 1], I32)
        tri = sb("tri", [P, P], BF16)
        stats = sb("stats", [P, KC, GROUPS, 6], F32)
        vec = sb("vec", [P, 3, KC], F32)
        bn_mv = sb("bn_mv", [P, KC, 2], F32)
        bn_t = sb("bn_t", [P, 3, KC], F32)
        bn_scale = sb("bn_scale", [P, KC], F32)
        bn_bias = sb("bn_bias", [P, KC], F32)
        eps_c = sb("eps_c", [P, 1], F32)

        one = ExitStack()
        s1 = allocator(one)
        vals = s1("vals", [P, WIN, TILES + 1, 6], BF16)
        slot1 = s1("slot1", [P, WIN, TILES + 1], F32)
        dl = s1("dl", [P, WIN, TILES + 1], F32)
        xT_raw = s1("xT_raw", [P, 2, KC, GR], F32)
        wT = {(m, part): s1(f"w{m}T_{part}", [P, KC, D], F32R) for m in "lr" for part in ("hi", "lo")}
        xT_hi = s1("xT_hi", [P, 2, KC, GR], F32R)
        xT_lo = s1("xT_lo", [P, 2, KC, GR], F32R)

        zero = ExitStack()
        s0 = allocator(zero, "right")
        w_raw = s0("w_raw", [P, 2, KC, D], F32)
        ends = s0("ends", [BP, 2, BC, EB], I32)
        part_i = s0("part_i", [BP, 4, BC, EB], I32)
        part_b = s0("part_b", [BP, 4, BC, EB], BF16)
        last_f = s0("last_f", [BP, BC], F32)
        d128 = s0("d128", [P, TILES], F32)
        d128_1 = s0("d128_1", [P, TILES], F32)
        before = s0("before", [BP, BC, TILES], BF16)
        first_b = s0("first_b", [P, TILES], F32)
        block_id = s0("block_id", [P, BC, WIN], F32)
        pick = s0("pick", [BP, WIN, BC, TILES], BF16)
        tmp = s0("tmp", [P, 5, TILES], F32)
        in_tile = s0("in_tile", [P, WIN, TILES], F32)
        member = s0("member", [P, WIN, TILES], BF16)
        covered = s0("covered", [P, 2], F32)
        left_f = s0("left_f", [P, 1], F32)
        part_no = s0("part_no", [P, 1], F32)
        row_i = s0("row_i", [P, 3, WIN, TILES], I32)
        e_src = s0("e_src", [P, 1], U32)
        e_dst = s0("e_dst", [P, 1], U32)
        e_row = s0("e_row", [P, P], U32)
        e_dst_f = s0("e_dst_f", [P, 1], F32)
        e_row_f = s0("e_row_f", [P, P], F32)
        same = s0("same", [P, P], F32)
        earlier = s0("earlier", [P, P], F32)
        repeated = s0("repeated", [P, 1], F32)
        e_write = s0("e_write", [P, 1], U32)
        e_x = s0("e_x", [P, CW], F32)
        e_sum = s0("e_sum", [P, CW], F32)
        e_count = s0("e_count", [P, 1], F32)
        zero.close()

        both = allocator(ctx, "right")
        xs = both("xs", [P, 2, GT, D], F32)
        h_out = both("h_out", [P, 2, KC, GR], F32)

        hot_slot = s1("hot_slot", [P, 2, WIN, P], BF16)
        hot_dst = s1("hot_dst", [P, 2, WIN, P], BF16)
        ct = s1("ct", [P, 4, 8], F32)
        idx_u = s1("idx_u", [P, 4, 1], U32)
        spread = s1("spread", [P, 4, P], F32R)
        rows = s1("rows", [P, 2, D], F32)
        rows_hi = s1("rows_hi", [P, 2, D], F32R)
        rows_lo = s1("rows_lo", [P, 2, D], F32R)
        x_self = s1("x_self", [P, 2, D], F32)
        aggr = s1("aggr", [P, 2, D], F32)
        aT_hi = s1("aT_hi", [P, 2, KC, GR], F32R)
        aT_lo = s1("aT_lo", [P, 2, KC, GR], F32R)
        one.close()

        two = ExitStack()
        s2 = allocator(two)
        x_early = s2("x_early", [P, EARLY, GT, D], F32)
        h_early = s2("h_early", [P, EARLY, KC, GR], F32)
        x_late = s2("x_late", [P, H2 - KEPT - EARLY, GT, D], F32)
        h_late = s2("h_late", [P, H2 - KEPT - EARLY, KC, GR], F32)
        r2 = s2("r2", [P, 2, KC, GR], F32)
        o2 = s2("o2", [P, OB, GT, D], F32)
        st2 = s2("st2", [P, 2, GT, 6], F32)
        mv2 = s2("mv2", [P, 2, GT, 2], F32)
        sd2 = s2("sd2", [P, 2, GT, 1], F32)
        rs2 = s2("rs2", [P, 2, GT, 1], F32)
        nm2 = s2("nm2", [P, 2, GT, 1], F32)
        two.close()
        x2 = [t[:, b] for t in (xs, x_early, x_late) for b in range(t.shape[1])]
        h2 = [t[:, b] for t in (h_out, h_early, h_late) for b in range(t.shape[1])]

        ph = [ps(f"ph{i}", [P, GR]) for i in range(4)]
        paT = [ps(f"paT{i}", [P, KC * P]) for i in range(2)]
        pagg = ps("pagg", [P, D])
        pslot = ps("pslot", [P, 512])
        pwin = [*paT, pagg, pslot]

        s_w = [sem(f"w{m}_loaded") for m in "lr"]
        s_ends = sem("ends_loaded")
        s_vec = sem("vec_loaded")
        s_const = sem("constants_ready")
        s_p0 = sem("prep_vector")
        s_pool0 = sem("pool_step")
        s_wa = sem("windows_copied")
        s_wh = sem("w_hi")
        s_wl = sem("w_lo")
        s_first = sem("first_blocks")
        s_win = sem("windows_picked")
        s_wu = sem("windows_read")
        s_rank = sem("ranks_summed")
        s_pv = sem("prep_vector_step")
        s_gv = sem("general_vector_step")
        s_tab = sem("tables_ready")
        s_cov = sem("covered_counted")
        s_covs = sem("covered_summed")
        s_flag = sem("left_over_ready")
        s_zero = sem("zeros_ready")
        s_zf = sem("sums_cleared")
        s_blk = sem("block_free")
        s_sl = sem("edges_loaded")
        s_eq = sem("same_row_steps")
        s_er = sem("repeats_found")
        s_sg = sem("sources_gathered")
        s_ss = sem("sums_gathered")
        s_sp = sem("block_summed")
        s_sa = sem("sums_added")
        s_sc = sem("sums_scattered")
        s_ml = sem("sums_loaded")
        s_mc = sem("mean_steps")
        s_mm = sem("means_ready")
        s_ms = sem("means_stored")
        s_mnext = sem("means_written")
        s_mdone = sem("general_path_done")
        s_x = [sem(f"x_loaded{b}") for b in range(2)]
        s_xp = sem("x_part_loaded")
        s_xt = [sem(f"xT_loaded{b}") for b in range(2)]
        s_hot = sem("one_hots_built")
        s_comp = sem("slots_filled")
        s_is = sem("slot_steps")
        s_idx = sem("indices_ready")
        s_gat = [sem(f"rows_gathered{b}") for b in range(2)]
        s_go = sem("gather_allowed")
        s_gh = sem("rows_hi_ready")
        s_gl = sem("rows_lo_ready")
        s_agg = sem("rows_summed")
        s_xself = sem("x_self_ready")
        s_aggr = sem("aggr_ready")
        s_xh = sem("xT_hi_ready")
        s_xl = sem("xT_lo_ready")
        s_atr = sem("aggr_transposed")
        s_ah = sem("aT_hi_ready")
        s_al = sem("aT_lo_ready")
        s_main = sem("h_summed")
        s_hc = sem("h_copied")
        s_bn = sem("h_counted")
        s_st = [sem(f"h_stored{b}") for b in range(2)]
        s_stfree = sem("h_out_free")
        s_mz = sem("moments_cleared")
        s_bnv = sem("bn_vector")
        s_bns = sem("bn_root")
        s_bnr = sem("bn_ready")
        s_h2 = [sem(f"h2_loaded{b}") for b in range(H2)]
        s_x2 = [sem(f"x2_loaded{b}") for b in range(H2)]
        s_relu = sem("relu_ready")
        s_t2 = sem("relu_transposed")
        s_y = sem("y_ready")
        s_m1 = sem("tile_counted")
        s_all = sem("group_counted")
        s_m2 = sem("moments_ready")
        s_sd = sem("deviation_ready")
        s_rs = sem("inverse_ready")
        s_oa = sem("normalised_by_act")
        s_od = sem("normalised_by_dve")
        s_os = [sem(f"out_stored{b}") for b in range(OB)]

        block = ctx.enter_context(nc.Block())

        @block.sync
        def _(sp):
            def load_xT(g, b):
                if isinstance(g, int) and (g + 1) * GR > N:
                    sp.dma_start(xT_raw[:, b, :, 0:N - g * GR], xT_part).then_inc(s_xt[b], 16)
                else:
                    sp.dma_start(xT_raw[:, b], xT_whole[g]).then_inc(s_xt[b], 16)

            sp.dma_start(ends[:, 0], src.rearrange("(c b p) -> b c p", b=BP, p=EB)).then_inc(s_ends, 16)
            sp.dma_start(ends[:, 1], dst.rearrange("(c b p) -> b c p", b=BP, p=EB)).then_inc(s_ends, 16)
            for m, w in ((1, wT_r), (0, wT_l)):
                sp.dma_start(w_raw[:, m], w.rearrange("(c p) f -> p c f", p=P)).then_inc(s_w[m], 16)
            with nc.allow_non_contiguous_dma(reason="three short vectors"):
                for m, v in enumerate((b_l, gamma, beta)):
                    sp.dma_start(vec[:, m], v.rearrange("(c p) -> p c", p=P)).then_inc(s_vec, 16)
            load_xT(0, 0)
            load_xT(1, 1)

            def load_x(g, b):
                if isinstance(g, int) and (g + 1) * GR > N:
                    full = (N - g * GR) // P
                    lot = sp.dma_start(xs[:, b, 0:full],
                                       x[g * GR:g * GR + full * P, :].rearrange("(t p) f -> p t f", p=P))
                    lot.then_inc(s_x[b], 16)
                    sp.dma_start(xs[0:LAST_ROWS, b, full], x[N - LAST_ROWS:N, :]).then_inc(s_xp, 16)
                else:
                    sp.dma_start(xs[:, b], x_group(g)).then_inc(s_x[b], 16)

            sp.wait_ge(s_wl, 2 * KC)
            load_x(0, 0)
            load_x(1, 1)
            sp.wait_ge(s_flag, 1)
            with sp.If(sp.value_load(left_over[0:1, 0:1], min_val=0, max_val=E) > 0):
                sp.wait_ge(s_zero, 1)
                with sp.Fori(0, TILES - 1) as d:
                    sp.dma_start(sum_dram[bass.ds(d * P, P), :], e_sum[:]).then_inc(s_zf, 16)
                sp.dma_start(sum_dram[N - LAST_ROWS:N, :], e_sum[0:LAST_ROWS, :]).then_inc(s_zf, 16)
                sp.wait_ge(s_zf, 16 * TILES)
                sp.sem_inc(s_blk, 1)
                with sp.Fori(0, NB) as n:
                    sp.wait_ge(s_blk, n + 1)
                    with nc.allow_non_contiguous_dma(reason="an edge to a partition"):
                        for t, e in ((e_src, src), (e_dst, dst)):
                            sp.dma_start(t[0:EB, :], e.bitcast(U32)[bass.ds(n * EB, EB)]
                                         .rearrange("(p o) -> p o", o=1)).then_inc(s_sl, 16)
                    sp.dma_start(e_row[0:EB, 0:EB], dst.bitcast(U32)[bass.ds(n * EB, EB)]
                                 .rearrange("(o p) -> o p", o=1).to_broadcast([EB, EB])).then_inc(s_sl, 16)
                sp.wait_ge(s_blk, NB + 1)

                def mean_tile(d, n):
                    rows = bass.ds(d * P, n)
                    sp.dma_start(e_sum[0:n, :], sum_dram[rows, :]).then_inc(s_ml, 16)
                    sp.wait_ge(s_mm, d + 1)
                    sp.dma_start(mean_dram[rows, :], e_x[0:n, 0:D]).then_inc(s_ms, 16)
                    sp.wait_ge(s_ms, 16 * d + 16)
                    sp.sem_inc(s_mnext, 1)

                with sp.Fori(0, TILES - 1) as d:
                    mean_tile(d, P)
                mean_tile(TILES - 1, LAST_ROWS)
                sp.sem_inc(s_mdone, 1)
            sp.wait_ge(s_tab, 1)

            def group(g, b, after):
                if after:
                    sp.wait_ge(s_xself, GT * g + GT)
                    load_x(g + 2, b)
                    sp.wait_ge(s_xl, GT * g + GT)
                    load_xT(g + 2, b)
                if isinstance(g, int) and g >= GROUPS - KEPT:
                    return
                sp.wait_ge(s_hc, GT * g + 4 + GT)
                sp.dma_start(h_dram[g], h_out[:, b]).then_inc(s_st[b], 16)
                sp.wait_ge(s_st[b], 8 * (g - b) + 16)
                sp.sem_inc(s_stfree, 1)

            if PAIRS > 1:
                with sp.Fori(0, PAIRS - 1) as q:
                    for b in range(2):
                        group(2 * q + b, b, True)
            for g in range(2 * PAIRS - 2, GROUPS):
                group(g, g % 2, g + 2 < GROUPS)

            def load2(k, b):
                g = group_of(k)
                sp.dma_start(h2[b], h_dram[g]).then_inc(s_h2[b], 16)
                sp.dma_start(x2[b], x_group(g)).then_inc(s_x2[b], 16)

            def store2(k, b):
                g = group_of(k)
                sp.wait_ge(s_oa, 2 * k + 2)
                sp.wait_ge(s_od, 2 * k + 2)
                if cols_of(k) < GR:
                    full = cols_of(k) // P
                    sp.dma_start(out[g * GR:g * GR + full * P, :].rearrange("(t p) f -> p t f", p=P),
                                 o2[:, b, 0:full]).then_inc(s_os[b], 16)
                    sp.dma_start(out[N - LAST_ROWS:N, :], o2[0:LAST_ROWS, b, full]).then_inc(s_os[b], 16)
                else:
                    sp.dma_start(out[bass.ds(g * GR, GR), :].rearrange("(t p) f -> p t f", p=P),
                                 o2[:, b]).then_inc(s_os[b], 16)

            sp.wait_ge(s_comp, TILES)
            sp.wait_ge(s_xl, GROUPS * GT)
            for k in range(KEPT, KEPT + EARLY):
                load2(k, k)
            sp.wait_ge(s_main, GROUPS * GT)
            for k in range(KEPT + EARLY, H2):
                load2(k, k)
            for k in range(H2):
                store2(k, k % OB)
                load2(k + H2, k)
            rounds2 = (GROUPS - H2) // H2
            if rounds2 > 1:
                with sp.Fori(1, rounds2) as q:
                    for k in range(H2):
                        store2(H2 * q + k, k % OB)
                        load2(H2 * q + (k + H2), k)
            for k in range(H2 * max(rounds2, 1), GROUPS):
                store2(k, k % OB)
                if k + H2 < GROUPS:
                    load2(k + H2, k % H2)
            for b in range(OB):
                stores = len(range(b, GROUPS, OB)) + (b == KEPT - 1)
                sp.wait_ge(s_os[b], 16 * stores)

        @block.tensor
        def _(pe):
            def product(base, c, m, hi, lo, first):
                b, fc = c // GT % 2, c % GT
                u = base + c
                cols = GR
                if isinstance(base, int):
                    cols = min(GR, N - (u // GT) * GR)
                for kc in range(KC):
                    for part, side in (("hi", hi), ("hi", lo), ("lo", hi)):
                        done = not first and kc == KC - 1 and part == "lo"
                        last = pe.matmul(ph[fc][:, 0:cols], wT[m, part][:, kc, fc * P:(fc + 1) * P],
                                         side[:, b, kc, 0:cols],
                                         start=first and kc == 0 and part == "hi" and side is hi, stop=done)
                return last

            pe.wait_ge(s_const, 2)
            pe.wait_ge(s_p0, 1)
            for c in range(BC):
                last = pe.matmul(pslot[:, 0:TILES], ones_b[0:BP, :], before[:, c, :], start=c == 0, stop=c == BC - 1)
            last.then_inc(s_first, 1)
            for j in range(WIN):
                pe.wait_ge(s_p0, 2 + j)
                if j > 0:
                    pe.wait_ge(s_wu, 2 * j)
                    pe.wait_ge(s_wa, 3 * j)
                for a in range(4):
                    for c in range(BC):
                        last = pe.matmul(pwin[a][0:EB, 0:TILES], part_b[:, a, c, :], pick[:, j, c, :],
                                         start=c == 0, stop=c == BC - 1)
                last.then_inc(s_win, 1)
                if j == 0:
                    pe.wait_ge(s_wl, KC)
                    pe.wait_ge(s_xl, GT)
                product(0, j, "r", xT_hi, xT_lo, True)
            pe.wait_ge(s_p0, 2 + WIN)
            pe.wait_ge(s_wa, 3 * WIN)
            for j in range(WIN):
                last = pe.matmul(pwin[j][0:EB, 0:TILES], tri[0:EB, 0:EB], member[0:EB, j, :], start=True, stop=j == 0)
                for k in range(j):
                    last = pe.matmul(pwin[j][0:EB, 0:TILES], ones_b[0:EB, 0:EB], member[0:EB, k, :], start=False,
                                     stop=k == j - 1)
            last.then_inc(s_rank, 1)
            for j in range(WIN, KC):
                product(0, j, "r", xT_hi, xT_lo, True)
            pe.wait_ge(s_cov, 1)
            pe.matmul(pslot[0:1, 0:1], covered[0:EB, 0:1], ones_f[0:EB, :], start=True, stop=True).then_inc(s_covs, 1)
            pe.wait_ge(s_flag, 1)
            with pe.If(pe.value_load(left_over[0:1, 0:1], min_val=0, max_val=E) > 0):
                with pe.Fori(0, NB) as n:
                    pe.wait_ge(s_eq, 3 * n + 2)
                    pe.wait_ge(s_sg, 16 * n + 16)
                    pe.matmul(pagg[0:EB, :], same[0:EB, 0:EB], e_x[0:EB, 0:D], start=True, stop=True)
                    pe.matmul(pslot[0:EB, 0:CW - D], same[0:EB, 0:EB], e_x[0:EB, D:CW], start=True,
                              stop=True).then_inc(s_sp, 1)
            pe.wait_ge(s_tab, 1)

            def fill_slots(base, c):
                i = base + c
                b = c % 2
                pe.wait_ge(s_hot, i + 1)
                if not (isinstance(i, int) and i == 0):
                    pe.wait_ge(s_is, 4 * i - 3)
                for j in range(WIN):
                    pe.matmul(pslot[:, 0:3], hot_slot[0:EB, b, j, :], vals[0:EB, j, i, 0:3],
                              start=j == 0, stop=j == WIN - 1)
                for j in range(WIN):
                    last = pe.matmul(pslot[:, 3:5], hot_dst[0:EB, b, j, :], vals[0:EB, j, i, 3:5],
                                     start=j == 0, stop=j == WIN - 1)
                last.then_inc(s_comp, 1)

            def sum_rows(base, c):
                i = base + c
                b = c % 2
                pe.wait_ge(s_gl, i + 1)
                pe.wait_ge(s_idx, i + 1)
                if not (isinstance(i, int) and i == 0):
                    pe.wait_ge(s_aggr, i)
                pe.matmul(pagg[:], spread[:, c % 4, :], rows_hi[:, b, :], start=True, stop=False)
                pe.matmul(pagg[:], spread[:, c % 4, :], rows_lo[:, b, :], start=False, stop=True).then_inc(s_agg, 1)

            def transpose_aggr(base, c):
                i = base + c
                n = rows_of(i)
                pe.wait_ge(s_aggr, i + 1)
                if not (isinstance(i, int) and i < 2):
                    pe.wait_ge(s_al, i - 1)
                for kc in range(KC):
                    last = pe.transpose(paT[c % 2][:, kc * P:kc * P + n], aggr[0:n, c % 2, kc * P:(kc + 1) * P], ident[0:n, 0:n])
                last.then_inc(s_atr, 1)

            def slot(base, c, main):
                if exists(base + c + 7):
                    fill_slots(base, c + 7)
                if exists(base + c + 4):
                    transpose_aggr(base, c + 4)
                if exists(base + c + 5):
                    sum_rows(base, c + 5)
                u = base + c
                ready = GT * (c // GT) + GT + base
                if main and not (isinstance(u, int) and u < GT):
                    pe.wait_ge(s_hc, u + 1)
                    if c % GT == 0:
                        pe.wait_ge(s_xl, ready)
                    product(base, c, "r", xT_hi, xT_lo, True)
                if main:
                    if c == 0 and isinstance(base, int):
                        pe.wait_ge(s_wl, 2 * KC)
                    if c % GT == 0:
                        pe.wait_ge(s_al, min(ready, TILES) if isinstance(ready, int) else ready)
                    product(base, c, "l", aT_hi, aT_lo, False).then_inc(s_main, 1)

            for c in range(-8, LOOP):
                slot(0, c, c >= 0)
            with pe.Fori(1, PAIRS) as q:
                for c in range(LOOP):
                    slot(LOOP * q, c, True)
            for c in range(GROUPS * GT - REST):
                slot(REST, c, True)

            def back(g, b, cols):
                tiles = -(-cols // P)
                for t in range(tiles):
                    n = min(P, cols - t * P)
                    if t == 0:
                        pe.wait_ge(s_relu, GT * g + GT)
                    if not isinstance(g, int) or g > 0:
                        pe.wait_ge(s_y, GT * g + t - 3)
                    for fc in range(KC):
                        last = pe.transpose(ph[t][0:n, fc * P:(fc + 1) * P], r2[:, b, fc, t * P:t * P + n], ident[:])
                    last.then_inc(s_t2, 1 if t < tiles - 1 else GT - tiles + 1)

            for k in range(2):
                back(k, k, cols_of(k))
            with pe.Fori(1, PAIRS) as q:
                for b in range(2):
                    back(2 * q + b, b, GR)
            for k in range(2 * PAIRS, GROUPS):
                back(k, k % 2, GR)

        @block.scalar
        def _(act):
            def w_hi(m):
                act.wait_ge(s_w["lr".index(m)], 16)
                for kc in range(KC):
                    act.activation(wT[m, "hi"][:, kc, :], w_raw[:, "lr".index(m), kc, :], ACT.Copy).then_inc(s_wh, 1)

            def x_hi(base, c):
                i = base + c
                b, kc = c // GT % 2, c % GT
                cols = min(GR, N - (i // GT) * GR) if isinstance(i, int) else GR
                act.wait_ge(s_xt[b], 2 * base + 16 * (c // LOOP) + 16)
                if not (isinstance(i, int) and i < LOOP):
                    act.wait_ge(s_main, GT * (c // GT) + base - GT)
                act.activation(xT_hi[:, b, kc, 0:cols], xT_raw[:, b, kc, 0:cols], ACT.Copy).then_inc(s_xh, 1)

            w_hi("r")
            for c in range(GT):
                x_hi(0, c)
            w_hi("l")
            for j in range(WIN):
                act.wait_ge(s_win, j + 1)
                a = slice(0, EB)
                sh, slo, dh, dlo = (pwin[k][a, 0:TILES] for k in range(4))
                if j > 0:
                    act.wait_ge(s_wu, 2 * j)
                act.activation(tmp[a, 1], dlo, ACT.Copy).then_inc(s_wa, 1)
                act.activation(vals[a, j, 0:TILES, 0], sh, ACT.Copy, bias=-256.0)
                act.activation(tmp[a, 0], slo, ACT.Copy, bias=1.0).then_inc(s_wa, 1)
                act.activation(vals[a, j, 0:TILES, 1], slo, ACT.Copy).then_inc(s_wa, 1)
            act.sem_inc(s_hc, 4)
            act.sem_inc(s_stfree, 2)
            act.wait_ge(s_tab, 1)
            act.wait_ge(s_vec, 48)

            def self_share(base, c):
                i = base + c
                b, t, n = c // GT % 2, c % GT, rows_of(i)
                act.wait_ge(s_x[b], 2 * base + 16 * (c // LOOP) + 16)
                if n < P:
                    act.wait_ge(s_xp, 16)
                act.wait_ge(s_is, 4 * i + 4)
                if not (isinstance(i, int) and i < 2):
                    act.wait_ge(s_aggr, i - 1)
                act.activation(x_self[0:n, c % 2, :], xs[0:n, b, t, :], ACT.Copy,
                               scale=ct[0:n, c % 4, 7:8]).then_inc(s_xself, 1)

            def hi_of(base, c, bank, ready, side, done):
                i = base + c
                b, t, n = c // GT % 2, c % GT, rows_of(i)
                act.wait_ge(ready, i + 1)
                if not (isinstance(i, int) and i < LOOP):
                    act.wait_ge(s_main, GT * (c // GT) + base - GT)
                part = bank[c % 2][:, 0:KC * P].rearrange("p (c r) -> p c r", c=KC)[:, :, 0:n]
                act.activation(side[:, b, :, t * P:t * P + n], part, ACT.Copy).then_inc(done, 1)

            def rows_high(base, c):
                i = base + c
                if isinstance(i, int):
                    act.wait_ge(s_gat[c % 2], 16 * (i // 2 + 1))
                else:
                    act.wait_ge(s_gat[c % 2], 8 * base + 16 * (c // 2 + 1))
                if not (isinstance(i, int) and i < 2):
                    act.wait_ge(s_agg, i - 1)
                act.activation(rows_hi[:, c % 2, :], rows[:, c % 2, :], ACT.Copy).then_inc(s_gh, 1)

            def copy_h(base, c):
                u = base + c
                b, fc = c // GT % 2, c % GT
                cols = min(GR, N - (u // GT) * GR) if isinstance(base, int) else GR
                act.wait_ge(s_main, u + 1)
                if fc == 0:
                    g1 = c // GT + (base // GT if isinstance(base, int) else q2[0])
                    act.wait_ge(s_stfree, g1 + 1)
                    act.wait_ge(s_bn, GT * g1 + GT)
                act.activation(h_out[:, b, fc, 0:cols], ph[fc][:, 0:cols], ACT.Identity,
                               bias=vec[:, 0, fc:fc + 1]).then_inc(s_hc, 1)

            q2 = [0]

            def slot(base, c, main):
                if exists(base + c + 5):
                    self_share(base, c + 5)
                for k in x_chunks(base, c):
                    x_hi(base, k)
                if exists(base + c + 4):
                    hi_of(base, c + 4, paT, s_atr, aT_hi, s_ah)
                if exists(base + c + 6):
                    rows_high(base, c + 6)
                if main:
                    copy_h(base, c)

            for c in range(-8, LOOP):
                slot(0, c, c >= 0)
            with act.Fori(1, PAIRS) as q:
                q2[0] = 2 * q
                for c in range(LOOP):
                    slot(LOOP * q, c, True)
            for c in range(GROUPS * GT - REST):
                slot(REST, c, True)

            act.wait_ge(s_bnv, KC)
            act.activation(bn_t[:, 0, :], bn_mv[:, :, 1], ACT.Sqrt, bias=eps_c[:]).then_inc(s_bns, 1)
            act.wait_ge(s_bnr, 1)

            def relu(q, k):
                g, b, cols = H2 * q + k, k % 2, cols_of(H2 * q + k)
                if not isinstance(g, int) or g >= KEPT:
                    act.wait_ge(s_h2[k % H2], loaded(q, k))
                if not isinstance(g, int) or g >= 2:
                    act.wait_ge(s_t2, GT * g - GT)
                for fc in range(KC):
                    act.activation(r2[:, b, fc, 0:cols], h2[k % H2][:, fc, 0:cols], ACT.Relu,
                                   bias=bn_bias[:, fc:fc + 1], scale=bn_scale[:, fc:fc + 1]).then_inc(s_relu, 1)

            def root(g, k):
                b = k % 2
                act.wait_ge(s_m2, GT * g + GT)
                act.activation(sd2[:, b, :, 0], mv2[:, b, :, 1], ACT.Sqrt, bias=eps_c[:]).then_inc(s_sd, 1)

            def normalise(q, k):
                g, b, o = H2 * q + k, k % 2, k % OB
                act.wait_ge(s_rs, 2 * g + 2)
                if not isinstance(g, int) or g >= OB:
                    act.wait_ge(s_os[o], out_free(q, k))
                for t in range(2):
                    act.activation(o2[:, o, t, :], x2[k % H2][:, t, :], ACT.Identity, bias=nm2[:, b, t, :],
                                   scale=rs2[:, b, t, :]).then_inc(s_oa, 1)

            def step2(q, k):
                g = H2 * q + k
                if not isinstance(g, int) or g + 1 < GROUPS:
                    relu(q, k + 1)
                if not isinstance(g, int) or g > 0:
                    normalise(q, k - 1)
                if not isinstance(g, int) or g < GROUPS:
                    root(g, k)

            relu(0, 0)
            for k in range(H2):
                step2(0, k)
            if ROUNDS2 > 1:
                with act.Fori(1, ROUNDS2) as q:
                    for k in range(H2):
                        step2(q, k)
            for g in range(H2 * max(ROUNDS2, 1), GROUPS + 1):
                step2(g // H2, g % H2)

        @block.vector
        def _(dve):
            steps = {s_pv: 0, s_gv: 0}

            def link(ins, s=s_pv):
                steps[s] += 1
                ins.then_inc(s, 1)
                dve.wait_ge(s, steps[s])

            dve.memset(eps_c[:], EPS)
            dve.memset(vals[:, :, :, 3:4], 1.0)
            dve.memset(ones_f[:], 1.0)
            dve.wait_ge(s_ends, 32)
            dve.wait_ge(s_const, 2)
            link(dve.tensor_copy(last_f[:], ends[:, 1, :, EB - 1]))
            for c in range(BC):
                last = dve.tensor_scalar(before[:, c, :], d128[0:BP, :], last_f[:, c:c + 1], None, ALU.is_gt)
            last.then_inc(s_p0, 1)
            link(dve.tensor_scalar(part_i[:, 0], ends[:, 1], 1, None, ALU.add))
            link(dve.tensor_scalar(part_i[:, 2], part_i[:, 0], 8, None, ALU.logical_shift_right))
            link(dve.tensor_scalar(part_i[:, 3], part_i[:, 0], 255, None, ALU.bitwise_and))
            link(dve.tensor_scalar(part_i[:, 0], ends[:, 0], 8, None, ALU.logical_shift_right))
            link(dve.tensor_scalar(part_i[:, 1], ends[:, 0], 255, None, ALU.bitwise_and))
            link(dve.tensor_copy(part_b[:], part_i[:]))
            dve.wait_ge(s_first, 1)
            link(dve.tensor_copy(first_b[:], pslot[:, 0:TILES]))
            for j in range(WIN):
                for c in range(BC):
                    last = dve.tensor_scalar(pick[:, j, c, :], first_b[0:BP, :], block_id[0:BP, c, j:j + 1], None,
                                             ALU.is_equal)
                last.then_inc(s_p0, 1)
            a = slice(0, EB)
            for j in range(WIN):
                dve.wait_ge(s_wa, 3 * j + 1)
                dve.scalar_tensor_tensor(tmp[a, 3], pwin[2][a, 0:TILES], 256.0, tmp[a, 1],
                                         ALU.mult, ALU.add).then_inc(s_wu, 1)
                dve.wait_ge(s_wa, 3 * j + 2)
                dve.scalar_tensor_tensor(tmp[a, 2], pwin[0][a, 0:TILES], 256.0, tmp[a, 0],
                                         ALU.mult, ALU.add).then_inc(s_wu, 1)
                dve.wait_ge(s_wu, 2 * j + 2)
                dve.tensor_tensor(vals[a, j, 0:TILES, 4], tmp[a, 2], tmp[a, 3], ALU.is_equal)
                link(dve.tensor_tensor(dl[a, j, 0:TILES], tmp[a, 3], d128_1[a, :], ALU.subtract))
                dve.tensor_scalar(vals[a, j, 0:TILES, 2], dl[a, j, 0:TILES], float(P), None, ALU.subtract)
                link(dve.tensor_scalar(tmp[a, 4], dl[a, j, 0:TILES], 0.0, None, ALU.is_ge))
                link(dve.scalar_tensor_tensor(in_tile[a, j, :], dl[a, j, 0:TILES], float(P), tmp[a, 4],
                                              ALU.is_lt, ALU.mult))
                last = dve.scalar_tensor_tensor(member[a, j, :], vals[a, j, 0:TILES, 4], 0.5, in_tile[a, j, :],
                                                ALU.is_lt, ALU.mult)
            last.then_inc(s_p0, 1)
            dve.tensor_reduce(covered[a, 0:1], in_tile[a], AX.XY, ALU.add)
            dve.wait_ge(s_rank, 1)
            for j in range(WIN):
                last = dve.scalar_tensor_tensor(slot1[a, j, 0:TILES], pwin[j][a, 0:TILES], 1.0, member[a, j, :],
                                                ALU.add, ALU.mult)
            link(last)
            link(dve.tensor_reduce(covered[a, 1:2], slot1[a, :, 0:TILES], AX.XY, ALU.max))
            link(dve.tensor_scalar(covered[a, 1:2], covered[a, 1:2], float(P), None, ALU.is_gt))
            dve.tensor_tensor(covered[a, 0:1], covered[a, 0:1], covered[a, 1:2], ALU.subtract).then_inc(s_cov, 1)
            dve.wait_ge(s_covs, 1)
            link(dve.tensor_scalar(left_f[0:1, :], pslot[0:1, 0:1], -1.0, float(E), ALU.mult, ALU.add))
            dve.tensor_copy(left_over[0:1, :], left_f[0:1, :]).then_inc(s_flag, 1)
            dve.wait_ge(s_flag, 1)
            with dve.If(dve.value_load(left_over[0:1, 0:1], min_val=0, max_val=E) > 0):
                link(dve.memset(e_x[:], 1.0), s_gv)
                dve.memset(e_sum[:], 0.0).then_inc(s_zero, 1)
                with dve.Fori(0, NB) as n:
                    dve.wait_ge(s_sl, 48 * n + 48)
                    dve.tensor_copy(e_row_f[a, 0:EB], e_row[a, 0:EB])
                    dve.tensor_copy(e_dst_f[a], e_dst[a]).then_inc(s_eq, 1)
                    dve.wait_ge(s_eq, 3 * n + 1)
                    dve.tensor_scalar(same[a, 0:EB], e_row_f[a, 0:EB], e_dst_f[a], None, ALU.is_equal).then_inc(s_eq, 1)
                    dve.wait_ge(s_eq, 3 * n + 2)
                    dve.scalar_tensor_tensor(earlier[a, 0:EB], iota_0[a, 0:EB], part_no[a], same[a, 0:EB],
                                             ALU.is_lt, ALU.mult).then_inc(s_eq, 1)
                    dve.wait_ge(s_eq, 3 * n + 3)
                    dve.tensor_reduce(repeated[a], earlier[a, 0:EB], AX.X, ALU.max).then_inc(s_er, 1)
                    dve.wait_ge(s_er, n + 1)
                    dve.scalar_tensor_tensor(e_write[a], repeated[a], float(EMPTY), e_dst_f[a], ALU.mult, ALU.add)
                    dve.wait_ge(s_sp, n + 1)
                    dve.wait_ge(s_ss, 16 * n + 16)
                    dve.tensor_tensor(e_sum[a, 0:D], pagg[a, :], e_sum[a, 0:D], ALU.add)
                    dve.tensor_tensor(e_sum[a, D:CW], pslot[a, 0:CW - D], e_sum[a, D:CW], ALU.add).then_inc(s_sa, 1)

                def mean_tile(d, n):
                    dve.wait_ge(s_ml, 16 * d + 16)
                    dve.tensor_scalar(e_count[0:n], e_sum[0:n, D:D + 1], 1.0, None, ALU.max).then_inc(s_mc, 1)
                    dve.wait_ge(s_mc, 2 * d + 1)
                    dve.reciprocal(e_count[0:n], e_count[0:n]).then_inc(s_mc, 1)
                    dve.wait_ge(s_mc, 2 * d + 2)
                    dve.tensor_scalar(e_x[0:n, 0:D], e_sum[0:n, 0:D], e_count[0:n], None, ALU.mult).then_inc(s_mm, 1)

                with dve.Fori(0, TILES - 1) as d:
                    mean_tile(d, P)
                mean_tile(TILES - 1, LAST_ROWS)
                dve.wait_ge(s_mdone, 1)
                dve.tensor_scalar(row_i[a, 1], row_i[a, 0], 8, None, ALU.logical_shift_right)
                link(dve.tensor_scalar(row_i[a, 2], row_i[a, 0], 255, None, ALU.bitwise_and), s_gv)
                for j in range(WIN):
                    dve.tensor_scalar(vals[a, j, 0:TILES, 0], row_i[a, 1, j], 256.0, None, ALU.subtract)
                    dve.tensor_copy(vals[a, j, 0:TILES, 1], row_i[a, 2, j])
                    link(dve.tensor_copy(in_tile[a, j], row_i[a, 0, j]), s_gv)
                    link(dve.tensor_tensor(dl[a, j, 0:TILES], in_tile[a, j], d128[a, :], ALU.subtract), s_gv)
                    dve.tensor_scalar(vals[a, j, 0:TILES, 2], dl[a, j, 0:TILES], float(P), None, ALU.subtract)
                    dve.tensor_scalar(slot1[a, j, 0:TILES], dl[a, j, 0:TILES], 1.0, None, ALU.add)
                link(dve.memset(vals[:, :, :, 4:5], 0.0), s_gv)
            dve.wait_ge(s_wl, 2 * KC)
            dve.memset(slot1[:, :, TILES:TILES + 1], 0.0)
            dve.memset(dl[:, :, TILES:TILES + 1], -1.0).then_inc(s_tab, 1)
            dve.sem_inc(s_bn, 8)
            dve.wait_ge(s_tab, 1)

            def one_hots(base, c):
                i = base + c
                b = c % 2
                if not (isinstance(i, int) and i < 2):
                    dve.wait_ge(s_comp, i - 1)
                for j in range(WIN):
                    dve.tensor_scalar(hot_slot[a, b, j, :], iota_1[a, :], slot1[a, j, bass.ds(i, 1)], None, ALU.is_equal)
                for j in range(WIN):
                    last = dve.tensor_scalar(hot_dst[a, b, j, :], iota_0[a, :], dl[a, j, bass.ds(i, 1)], None, ALU.is_equal)
                last.then_inc(s_hot, 1)

            def indices(base, c):
                i = base + c
                k = c % 4
                dve.wait_ge(s_comp, i + 1)
                dve.tensor_copy(ct[:, k, 0:5], pslot[:, 0:5]).then_inc(s_is, 1)
                dve.wait_ge(s_is, 4 * i + 1)
                dve.scalar_tensor_tensor(ct[:, k, 5:6], ct[:, k, 0:1], 256.0, ct[:, k, 1:2], ALU.mult, ALU.add)
                dve.tensor_scalar(ct[:, k, 6:7], ct[:, k, 3:4], 1.0, None, ALU.max).then_inc(s_is, 1)
                dve.wait_ge(s_is, 4 * i + 2)
                dve.tensor_scalar(idx_u[:, k, :], ct[:, k, 5:6], float(EMPTY), None, ALU.add)
                dve.reciprocal(ct[:, k, 6:7], ct[:, k, 6:7]).then_inc(s_is, 1)
                dve.tensor_scalar(spread[:, k, :], iota_m[:], ct[:, k, 2:3], None, ALU.is_equal).then_inc(s_idx, 1)
                dve.wait_ge(s_is, 4 * i + 3)
                dve.tensor_tensor(ct[:, k, 7:8], ct[:, k, 4:5], ct[:, k, 6:7], ALU.mult).then_inc(s_is, 1)

            def mean(base, c):
                i = base + c
                n = rows_of(i)
                dve.wait_ge(s_agg, i + 1)
                dve.wait_ge(s_xself, i + 1)
                if not (isinstance(i, int) and i < 2):
                    dve.wait_ge(s_atr, i - 1)
                dve.scalar_tensor_tensor(aggr[0:n, c % 2, :], pagg[0:n, :], ct[0:n, c % 4, 6:7], x_self[0:n, c % 2, :],
                                         ALU.mult, ALU.add).then_inc(s_aggr, 1)

            def lo_of(base, c, bank, ready, hi, lo, done):
                i = base + c
                b, t, n = c // GT % 2, c % GT, rows_of(i)
                dve.wait_ge(ready, i + 1)
                part = bank[c % 2][:, 0:KC * P].rearrange("p (c r) -> p c r", c=KC)[:, :, 0:n]
                dve.tensor_tensor(lo[:, b, :, t * P:t * P + n], part,
                                  hi[:, b, :, t * P:t * P + n].bitcast(F32), ALU.subtract).then_inc(done, 1)

            def count_h(base, c):
                u = base + c
                fc = c % GT
                cols = min(GR, N - (u // GT) * GR) if isinstance(base, int) else GR
                g = c // GT + (base // GT if isinstance(base, int) else q2[0])
                dve.wait_ge(s_hc, u + 5)
                dve.bn_stats(stats[:, fc, g, :], h_out[:, c // GT % 2, fc, 0:cols]).then_inc(s_bn, 1)

            q2 = [0]

            def slot(base, c, main):
                if exists(base + c + 7):
                    indices(base, c + 7)
                if exists(base + c + 8):
                    one_hots(base, c + 8)
                if exists(base + c + 5):
                    mean(base, c + 5)
                if exists(base + c + 4):
                    lo_of(base, c + 4, paT, s_ah, aT_hi, aT_lo, s_al)
                if main:
                    count_h(base, c)

            for c in range(-8, 0):
                slot(0, c, False)
            with dve.Fori(0, PAIRS) as q:
                q2[0] = 2 * q
                for c in range(LOOP):
                    slot(LOOP * q, c, True)
            for c in range(GROUPS * GT - REST):
                slot(REST, c, True)
                fc = REST + c - (GROUPS - 1) * GT
                if fc >= 0:
                    dve.wait_ge(s_bn, (GROUPS - 1) * GT + fc + 1 + 8)
                    dve.bn_aggr(bn_mv[:, fc, :], stats[:, fc].rearrange("p g s -> p (g s)")).then_inc(s_bnv, 1)

            dve.wait_ge(s_vec, 48)
            dve.wait_ge(s_bns, 1)
            link(dve.reciprocal(bn_t[:, 1, :], bn_t[:, 0, :]))
            link(dve.tensor_tensor(bn_scale[:], bn_t[:, 1, :], vec[:, 1, :], ALU.mult))
            link(dve.tensor_tensor(bn_t[:, 2, :], bn_mv[:, :, 0], bn_scale[:], ALU.mult))
            dve.tensor_tensor(bn_bias[:], vec[:, 2, :], bn_t[:, 2, :], ALU.subtract).then_inc(s_bnr, 1)

            def sum_y(q, k):
                g, b, cols = H2 * q + k, k % 2, cols_of(H2 * q + k)
                tiles = -(-cols // P)
                x_in = x2[k % H2]
                if not isinstance(g, int) or g >= KEPT:
                    dve.wait_ge(s_x2[k % H2], loaded(q, k))
                for t in range(tiles):
                    n = min(P, cols - t * P)
                    dve.wait_ge(s_t2, GT * g + t + 1)
                    dve.tensor_tensor(x_in[0:n, t, :], ph[t][0:n, :], x_in[0:n, t, :],
                                      ALU.add).then_inc(s_y, 1 if t < tiles - 1 else GT - tiles + 1)
                if not isinstance(g, int) or g >= 2:
                    dve.wait_ge(s_oa, 2 * g - 2)
                for t in range(tiles):
                    n = min(P, cols - t * P)
                    dve.wait_ge(s_y, GT * g + t + 1)
                    dve.bn_stats(st2[0:n, b, t, :], x_in[0:n, t, :]).then_inc(
                        s_m1, 1 if t < tiles - 1 else GT - tiles + 1)
                dve.wait_ge(s_m1, GT * g + GT)
                dve.sem_inc(s_all, 1)
                for t in range(tiles):
                    n = min(P, cols - t * P)
                    last = dve.bn_aggr(mv2[0:n, b, t, :], st2[0:n, b, t, :])
                    last.then_inc(s_m2, 1 if t < tiles - 1 else GT - tiles + 1)

            def invert(g, k):
                b = k % 2
                dve.wait_ge(s_sd, g + 1)
                dve.reciprocal(rs2[:, b], sd2[:, b]).then_inc(s_rs, 1)
                dve.wait_ge(s_rs, 2 * g + 1)
                dve.scalar_tensor_tensor(nm2[:, b, :, 0], mv2[:, b, :, 0], -1.0, rs2[:, b, :, 0],
                                         ALU.mult, ALU.mult).then_inc(s_rs, 1)

            def normalise(q, k):
                g, b, o = H2 * q + k, k % 2, k % OB
                dve.wait_ge(s_rs, 2 * g + 2)
                if not isinstance(g, int) or g >= OB:
                    dve.wait_ge(s_os[o], out_free(q, k))
                tiles = -(-cols_of(g) // P)
                for t in range(2, tiles):
                    n = min(P, cols_of(g) - t * P)
                    dve.tensor_scalar(o2[0:n, o, t, :], x2[k % H2][0:n, t, :], mv2[0:n, b, t, 0:1],
                                      rs2[0:n, b, t, :], ALU.subtract, ALU.mult).then_inc(
                                          s_od, 1 if t < tiles - 1 else GT - tiles + 1)

            def step2(q, k):
                g = H2 * q + k
                if not isinstance(g, int) or g < GROUPS:
                    sum_y(q, k)
                if not isinstance(g, int) or g > 0:
                    normalise(q, k - 1)
                if not isinstance(g, int) or g < GROUPS:
                    invert(g, k)

            dve.memset(mv2[:], 1.0).then_inc(s_mz, 1)
            dve.wait_ge(s_mz, 1)
            for b in range(KEPT):
                dve.wait_ge(s_x[b], 8 * GROUPS)
            dve.wait_ge(s_xp, 16)
            for k in range(H2):
                step2(0, k)
            if ROUNDS2 > 1:
                with dve.Fori(1, ROUNDS2) as q:
                    for k in range(H2):
                        step2(q, k)
            for g in range(H2 * max(ROUNDS2, 1), GROUPS + 1):
                step2(g // H2, g % H2)

        @block.gpsimd
        def _(pool):
            def number(t, pattern, base, channel):
                return pool.iota(t, pattern, base=base, channel_multiplier=channel, allow_small_or_imprecise_dtypes=True)

            pool.memset(ident[:], 0.0)
            pool.memset(tri[:], 1.0)
            pool.memset(ones_b[:], 1.0).then_inc(s_pool0, 1)
            pool.wait_ge(s_pool0, 1)
            pool.affine_select(out=ident[:], in_=ident[:], compare_op=ALU.not_equal, fill=1.0, base=0,
                               pattern=[[-1, P]], channel_multiplier=1).then_inc(s_const, 1)
            pool.affine_select(out=tri[:], in_=tri[:], compare_op=ALU.is_gt, fill=0.0, base=0,
                               pattern=[[1, P]], channel_multiplier=-1)
            number(d128[:], [[P, TILES]], 0, 0)
            number(d128_1[:], [[P, TILES]], 1, 0)
            number(block_id[:], [[BP, BC], [-1, WIN]], 0, 1)
            number(row_i[:, 0], [[EB, WIN], [P, TILES]], 0, 1)
            number(part_no[:], [[0, 1]], 0, 1)
            number(iota_m[:], [[1, P]], -P, 0)
            number(iota_0[:], [[1, P]], 0, 0)
            number(iota_1[:], [[1, P]], 1, 0).then_inc(s_const, 1)

            def w_lo(m):
                for kc in range(KC):
                    pool.wait_ge(s_wh, ("rl".index(m)) * KC + kc + 1)
                    pool.tensor_tensor(wT[m, "lo"][:, kc, :], w_raw[:, "lr".index(m), kc, :],
                                       wT[m, "hi"][:, kc, :].bitcast(F32), ALU.subtract).then_inc(s_wl, 1)

            def x_lo(base, c):
                i = base + c
                b, kc = c // GT % 2, c % GT
                cols = min(GR, N - (i // GT) * GR) if isinstance(i, int) else GR
                pool.wait_ge(s_xh, i + 1)
                pool.tensor_tensor(xT_lo[:, b, kc, 0:cols], xT_raw[:, b, kc, 0:cols],
                                   xT_hi[:, b, kc, 0:cols].bitcast(F32), ALU.subtract).then_inc(s_xl, 1)

            w_lo("r")
            for c in range(GT):
                x_lo(0, c)
            w_lo("l")
            pool.wait_ge(s_flag, 1)
            left = pool.value_load(left_over[0:1, 0:1], min_val=0, max_val=E)

            def indexed(out, table, of, index, scatter=False):
                by = bass.IndirectOffsetOnAxis(ap=index, axis=0)
                return pool.indirect_dma_start(out=table if scatter else out, out_offset=by if scatter else None,
                                               in_=out if scatter else table, in_offset=None if scatter else by,
                                               bounds_check=of - 1, oob_is_err=False)

            with pool.If(left > 0):
                pool.wait_ge(s_zf, 16 * TILES)
                with pool.Fori(0, NB) as n:
                    pool.wait_ge(s_sl, 48 * n + 48)
                    pool.sem_inc(s_go, 1)
                    indexed(e_x[0:EB, 0:D], x[:, :], N, e_src[0:EB, :]).then_inc(s_sg, 16)
                    indexed(e_sum[0:EB, :], sum_dram[:, :], N, e_dst[0:EB, :]).then_inc(s_ss, 16)
                    pool.wait_ge(s_sa, n + 1)
                    pool.sem_inc(s_go, 1)
                    indexed(e_sum[0:EB, :], sum_dram[:, :], N, e_write[0:EB, :], scatter=True).then_inc(s_sc, 16)
                    pool.wait_ge(s_sc, 16 * n + 16)
                    pool.sem_inc(s_blk, 1)
            pool.wait_ge(s_tab, 1)
            pool.memset(rows[:], 0.0).then_inc(s_pool0, 1)
            pool.wait_ge(s_pool0, 2)

            last_row = pool.alloc_register("last_row")
            pool.reg_mov(last_row, N - 1)

            def gather(base, c):
                i = base + c
                pool.wait_ge(s_idx, i + 1)
                if not (isinstance(i, int) and i < 2):
                    pool.wait_ge(s_gl, i - 1)
                pool.sem_inc(s_go, 1)
                with pool.If(left > 0):
                    indexed(rows[:, c % 2, :], mean_dram[:, :], N, idx_u[:, c % 4, :]).then_inc(s_gat[c % 2], 16)
                with pool.Else():
                    indexed(rows[:, c % 2, :], x[:, :], N, idx_u[:, c % 4, :]).then_inc(s_gat[c % 2], 16)

            def rows_low(base, c):
                i = base + c
                pool.wait_ge(s_gh, i + 1)
                pool.tensor_tensor(rows_lo[:, c % 2, :], rows[:, c % 2, :], rows_hi[:, c % 2, :].bitcast(F32),
                                   ALU.subtract).then_inc(s_gl, 1)

            def slot(base, c):
                if exists(base + c + 7):
                    gather(base, c + 7)
                if exists(base + c + 6):
                    rows_low(base, c + 6)
                for k in x_chunks(base, c):
                    x_lo(base, k)

            for c in range(-8, 0):
                slot(0, c)
            with pool.Fori(0, PAIRS) as q:
                for c in range(LOOP):
                    slot(LOOP * q, c)
            for c in range(TILES - REST):
                slot(REST, c)


def kernel(**inputs):
    import numpy as np
    import concourse.bacc as bacc
    from concourse.bass_utils import run_bass_kernel_spmd

    x = inputs["x"]
    n, d = x.shape
    whole = n // GR * GR
    arrays = {
        "x": x,
        "xT_whole": x[:whole].reshape(n // GR, GR, d // P, P).transpose(0, 3, 2, 1),
        "xT_part": x[whole:].reshape(n - whole, d // P, P).transpose(2, 1, 0),
        "src": inputs["src"],
        "dst": inputs["dst"],
        "wT_l": inputs["L0_gnn_W_l"].T,
        "b_l": inputs["L0_gnn_b_l"],
        "wT_r": inputs["L0_gnn_W_r"].T,
        "gamma": inputs["L0_gnn_gamma"],
        "beta": inputs["L0_gnn_beta"],
    }
    arrays = {name: np.ascontiguousarray(a) for name, a in arrays.items()}
    nc = bacc.Bacc("TRN2", target_bir_lowering=False, num_devices=1)
    args = [nc.dram_tensor(name, a.shape, mybir.dt.from_np(a.dtype), kind="ExternalInput").ap()
            for name, a in arrays.items()]
    out = nc.dram_tensor("out", x.shape, F32, kind="ExternalOutput").ap()
    bass_sage_batchnorm_residual_layernorm_kernel(nc, *args, out)
    return run_bass_kernel_spmd(nc, [arrays], core_ids=[0]).results[0]["out"]
```
